# Optimizing a Trainium2 kernel written in Bass

```python
import numpy as np
import jax
import jax.numpy as jnp

def _softmax(x, axis=-1):
    return jax.nn.softmax(x, axis=axis)

def _gelu(x):
    return jax.nn.gelu(x, approximate=True)

def _silu(x):
    return jax.nn.silu(x)

def _sigmoid(x):
    return jax.nn.sigmoid(x)

def _layernorm(x, axis=-1, eps=1e-05):
    m = jnp.mean(x, axis=axis, keepdims=True)
    v = jnp.var(x, axis=axis, keepdims=True)
    return (x - m) / jnp.sqrt(v + eps)

def _scatter_add(tgt, idx, src, axis=0):
    return tgt.at[idx].add(src)

def _segment_sum(src, seg, n):
    return jax.ops.segment_sum(src, seg, n)
kernel_name = 'mk_prb_d2_jaxref_r8_f9c1cd'

def setup_inputs(seed: int=0):
    np.random.seed(seed)
    _w = jnp.asarray

    def _L0_attn_setup():
        import jax, jax.numpy as jnp
        import numpy as np
        D_MODEL = 128
        N_HEADS = 16
        D_LATENT = 32
        HEAD_DIM = D_MODEL // N_HEADS

        def apply_rope(x):
            B, T, H, D = x.shape
            inv_freq = 1.0 / 10000.0 ** (jnp.arange(0, D, 2, dtype=jnp.float32) / D)
            t = jnp.arange(T, dtype=jnp.float32)
            freqs = t[:, None] * inv_freq[None, :]
            sin_f = jnp.sin(freqs)[None, :, None, :]
            cos_f = jnp.cos(freqs)[None, :, None, :]
            x1, x2 = jnp.split(x, 2, axis=-1)
            return jnp.concatenate([x1 * cos_f - x2 * sin_f, x1 * sin_f + x2 * cos_f], axis=-1)
        key = jax.random.key(seed)
        ks = jax.random.split(key, 10)
        B, T = (4, 512)
        s = lambda fan_in: 1.0 / np.sqrt(fan_in)
        return {'x': jax.random.normal(ks[0], (B, T, D_MODEL), dtype=jnp.float32), 'Wq': jax.random.normal(ks[1], (D_MODEL, D_MODEL), dtype=jnp.float32) * s(D_MODEL), 'bq': jnp.zeros((D_MODEL,), jnp.float32), 'Wdown': jax.random.normal(ks[2], (D_MODEL, D_LATENT), dtype=jnp.float32) * s(D_MODEL), 'bdown': jnp.zeros((D_LATENT,), jnp.float32), 'Wup': jax.random.normal(ks[3], (D_LATENT, 2 * D_MODEL), dtype=jnp.float32) * s(D_LATENT), 'bup': jnp.zeros((2 * D_MODEL,), jnp.float32), 'Wout': jax.random.normal(ks[4], (D_MODEL, D_MODEL), dtype=jnp.float32) * s(D_MODEL), 'bout': jnp.zeros((D_MODEL,), jnp.float32)}
    _L0_attn_in = _L0_attn_setup()

    def _L0_ffn_setup():
        import jax, jax.numpy as jnp
        import numpy as np
        B, P, D, D_MLP, E, K = (2, 256, 128, 512, 8, 2)
        key = jax.random.key(seed)
        k_x, k_g, k_in, k_out = jax.random.split(key, 4)
        s_in = 1.0 / np.sqrt(D).astype(np.float32)
        s_out = 1.0 / np.sqrt(D_MLP).astype(np.float32)
        return {'x': jax.random.normal(k_x, (B, P, D), dtype=jnp.float32), 'W_gate': jax.random.normal(k_g, (D, E), dtype=jnp.float32) * s_in, 'W_in': jax.random.normal(k_in, (E, D, D_MLP), dtype=jnp.float32) * s_in, 'b_in': jnp.zeros((E, D_MLP), dtype=jnp.float32), 'W_out': jax.random.normal(k_out, (E, D_MLP, D), dtype=jnp.float32) * s_out, 'b_out': jnp.zeros((E, D), dtype=jnp.float32)}
    _L0_ffn_in = _L0_ffn_setup()

    def _L1_attn_setup():
        import jax, jax.numpy as jnp
        import numpy as np
        D_MODEL = 128
        KERNEL_SIZE = 128
        ORDER = 2
        B, T = (4, 256)

        def _layernorm(x, gamma, beta, eps=1e-05):
            mu = jnp.mean(x, axis=-1, keepdims=True)
            var = jnp.mean(jnp.square(x - mu), axis=-1, keepdims=True)
            return (x - mu) * jax.lax.rsqrt(var + eps) * gamma + beta

        def _fft_conv(y_bdt, kernel, T):
            K = kernel.shape[-1]
            kpad = jnp.pad(kernel, ((0, 0), (0, 0), (0, max(0, T - K))))[:, :, :T]
            n = 2 * T
            y_f = jnp.fft.rfft(y_bdt, n=n)
            k_f = jnp.fft.rfft(kpad, n=n)
            conv = jnp.fft.irfft(y_f * k_f, n=n)[:, :, :T]
            return conv
        key = jax.random.key(seed)
        ks = jax.random.split(key, 8)
        x = jax.random.normal(ks[0], (B, T, D_MODEL), dtype=jnp.float32)
        W_in = jax.random.normal(ks[1], (D_MODEL, D_MODEL * (ORDER + 1)), dtype=jnp.float32) * (1.0 / np.sqrt(D_MODEL))
        b_in = jnp.zeros((D_MODEL * (ORDER + 1),), dtype=jnp.float32)
        k0 = jax.random.normal(ks[2], (1, D_MODEL, KERNEL_SIZE), dtype=jnp.float32) * 0.02
        k1 = jax.random.normal(ks[3], (1, D_MODEL, KERNEL_SIZE), dtype=jnp.float32) * 0.02
        gamma = jnp.ones((D_MODEL,), dtype=jnp.float32)
        beta = jnp.zeros((D_MODEL,), dtype=jnp.float32)
        W_out = jax.random.normal(ks[4], (D_MODEL, D_MODEL), dtype=jnp.float32) * (1.0 / np.sqrt(D_MODEL))
        b_out = jnp.zeros((D_MODEL,), dtype=jnp.float32)
        return {'x': x, 'W_in': W_in, 'b_in': b_in, 'k0': k0, 'k1': k1, 'gamma': gamma, 'beta': beta, 'W_out': W_out, 'b_out': b_out}
    _L1_attn_in = _L1_attn_setup()

    def _L1_ffn_setup():
        import jax, jax.numpy as jnp
        import numpy as np
        EMBED_DIM = 128
        HIDDEN_DIM = 512
        NUM_EXPERTS = 8
        TOP_K = 2
        key = jax.random.key(seed)
        k_x, k_g, k_w1, k_w2 = jax.random.split(key, 4)
        x = jax.random.normal(k_x, (2, 64, EMBED_DIM), dtype=jnp.float32)
        gate_w = jax.random.normal(k_g, (NUM_EXPERTS, EMBED_DIM), dtype=jnp.float32) * (1.0 / np.sqrt(EMBED_DIM))
        w1 = jax.random.normal(k_w1, (NUM_EXPERTS, EMBED_DIM, HIDDEN_DIM), dtype=jnp.float32) * np.sqrt(2.0 / EMBED_DIM)
        b1 = jnp.zeros((NUM_EXPERTS, HIDDEN_DIM), dtype=jnp.float32)
        w2 = jax.random.normal(k_w2, (NUM_EXPERTS, HIDDEN_DIM, EMBED_DIM), dtype=jnp.float32) * np.sqrt(2.0 / HIDDEN_DIM)
        b2 = jnp.zeros((NUM_EXPERTS, EMBED_DIM), dtype=jnp.float32)
        return {'x': x, 'gate_w': gate_w, 'w1': w1, 'b1': b1, 'w2': w2, 'b2': b2}
    _L1_ffn_in = _L1_ffn_setup()
    _d = {'L0_attn_x': _L0_attn_in['x'], 'L0_attn_Wq': _L0_attn_in['Wq'], 'L0_attn_bq': _L0_attn_in['bq'], 'L0_attn_Wdown': _L0_attn_in['Wdown'], 'L0_attn_bdown': _L0_attn_in['bdown'], 'L0_attn_Wup': _L0_attn_in['Wup'], 'L0_attn_bup': _L0_attn_in['bup'], 'L0_attn_Wout': _L0_attn_in['Wout'], 'L0_attn_bout': _L0_attn_in['bout'], 'L0_ffn_W_gate': _L0_ffn_in['W_gate'], 'L0_ffn_W_in': _L0_ffn_in['W_in'], 'L0_ffn_b_in': _L0_ffn_in['b_in'], 'L0_ffn_W_out': _L0_ffn_in['W_out'], 'L0_ffn_b_out': _L0_ffn_in['b_out'], 'L1_attn_W_in': _L1_attn_in['W_in'], 'L1_attn_b_in': _L1_attn_in['b_in'], 'L1_attn_k0': _L1_attn_in['k0'], 'L1_attn_k1': _L1_attn_in['k1'], 'L1_attn_gamma': _L1_attn_in['gamma'], 'L1_attn_beta': _L1_attn_in['beta'], 'L1_attn_W_out': _L1_attn_in['W_out'], 'L1_attn_b_out': _L1_attn_in['b_out'], 'L1_ffn_gate_w': _L1_ffn_in['gate_w'], 'L1_ffn_w1': _L1_ffn_in['w1'], 'L1_ffn_b1': _L1_ffn_in['b1'], 'L1_ffn_w2': _L1_ffn_in['w2'], 'L1_ffn_b2': _L1_ffn_in['b2']}
    _x0 = _d['L0_attn_x']
    _d['L0_attn_x'] = jax.random.normal(jax.random.fold_in(jax.random.key(seed), 1), (32, 256, 128), dtype=_x0.dtype)
    del _x0
    return _d

def reference(L0_attn_x, L0_attn_Wq, L0_attn_bq, L0_attn_Wdown, L0_attn_bdown, L0_attn_Wup, L0_attn_bup, L0_attn_Wout, L0_attn_bout, L0_ffn_W_gate, L0_ffn_W_in, L0_ffn_b_in, L0_ffn_W_out, L0_ffn_b_out, L1_attn_W_in, L1_attn_b_in, L1_attn_k0, L1_attn_k1, L1_attn_gamma, L1_attn_beta, L1_attn_W_out, L1_attn_b_out, L1_ffn_gate_w, L1_ffn_w1, L1_ffn_b1, L1_ffn_w2, L1_ffn_b2):

    def _L0_attn_ref(x, Wq, bq, Wdown, bdown, Wup, bup, Wout, bout):
        import jax, jax.numpy as jnp
        import numpy as np
        D_MODEL = 128
        N_HEADS = 16
        D_LATENT = 32
        HEAD_DIM = D_MODEL // N_HEADS

        def apply_rope(x):
            B, T, H, D = x.shape
            inv_freq = 1.0 / 10000.0 ** (jnp.arange(0, D, 2, dtype=jnp.float32) / D)
            t = jnp.arange(T, dtype=jnp.float32)
            freqs = t[:, None] * inv_freq[None, :]
            sin_f = jnp.sin(freqs)[None, :, None, :]
            cos_f = jnp.cos(freqs)[None, :, None, :]
            x1, x2 = jnp.split(x, 2, axis=-1)
            return jnp.concatenate([x1 * cos_f - x2 * sin_f, x1 * sin_f + x2 * cos_f], axis=-1)
        B, T, D = x.shape
        H, Dh = (N_HEADS, HEAD_DIM)
        q = x @ Wq + bq
        kv_latent = x @ Wdown + bdown
        kv = kv_latent @ Wup + bup
        q = q.reshape(B, T, H, Dh)
        kv = kv.reshape(B, T, H, 2 * Dh)
        k, v = jnp.split(kv, 2, axis=-1)
        q = apply_rope(q)
        k = apply_rope(k)
        att = jnp.einsum('bthd,btgd->bthg', q, k) / jnp.sqrt(jnp.float32(Dh))
        att = jax.nn.softmax(att, axis=-1)
        out = jnp.einsum('bthg,btgd->bthd', att, v)
        out = out.reshape(B, T, D)
        return out @ Wout + bout

    def _L0_ffn_ref(x, W_gate, W_in, b_in, W_out, b_out):
        import jax, jax.numpy as jnp
        import numpy as np
        B, P, D, D_MLP, E, K = (2, 256, 128, 512, 8, 2)
        gate_logits = jnp.einsum('bpd,de->bpe', x, W_gate)
        top_w, top_idx = jax.lax.top_k(gate_logits, K)
        top_w = jax.nn.softmax(top_w, axis=-1)
        combine = jnp.einsum('bpke,bpk->bpe', jax.nn.one_hot(top_idx, E, dtype=x.dtype), top_w)
        out = jnp.zeros_like(x)
        for e in range(E):
            h = jax.nn.gelu(jnp.einsum('bpd,dm->bpm', x, W_in[e]) + b_in[e], approximate=False)
            y = jnp.einsum('bpm,md->bpd', h, W_out[e]) + b_out[e]
            out = out + combine[..., e, None] * y
        return out

    def _L1_attn_ref(x, W_in, b_in, k0, k1, gamma, beta, W_out, b_out):
        import jax, jax.numpy as jnp
        import numpy as np
        D_MODEL = 128
        KERNEL_SIZE = 128
        ORDER = 2
        B, T = (4, 256)

        def _layernorm(x, gamma, beta, eps=1e-05):
            mu = jnp.mean(x, axis=-1, keepdims=True)
            var = jnp.mean(jnp.square(x - mu), axis=-1, keepdims=True)
            return (x - mu) * jax.lax.rsqrt(var + eps) * gamma + beta

        def _fft_conv(y_bdt, kernel, T):
            K = kernel.shape[-1]
            kpad = jnp.pad(kernel, ((0, 0), (0, 0), (0, max(0, T - K))))[:, :, :T]
            n = 2 * T
            y_f = jnp.fft.rfft(y_bdt, n=n)
            k_f = jnp.fft.rfft(kpad, n=n)
            conv = jnp.fft.irfft(y_f * k_f, n=n)[:, :, :T]
            return conv
        Bn, Tn, Dn = x.shape
        residual = x
        xn = _layernorm(x, gamma, beta)
        proj = (xn @ W_in + b_in).reshape(Bn, Tn, ORDER + 1, Dn)
        v = proj[:, :, 0, :]
        y = jnp.transpose(v, (0, 2, 1))
        for i, kern in enumerate((k0, k1)):
            xi = jnp.transpose(proj[:, :, i + 1, :], (0, 2, 1))
            y = _fft_conv(y, kern, Tn) * xi
        y = jnp.transpose(y, (0, 2, 1))
        y = y @ W_out + b_out
        return residual + y

    def _L1_ffn_ref(x, gate_w, w1, b1, w2, b2):
        import jax, jax.numpy as jnp
        import numpy as np
        EMBED_DIM = 128
        HIDDEN_DIM = 512
        NUM_EXPERTS = 8
        TOP_K = 2
        orig_shape = x.shape
        xt = x.reshape(-1, EMBED_DIM)
        logits = xt @ gate_w.T
        probs = jax.nn.softmax(logits, axis=-1)
        top_w, top_i = jax.lax.top_k(probs, TOP_K)
        top_w = top_w / (top_w.sum(axis=-1, keepdims=True) + 1e-09)
        h = jnp.einsum('td,ndh->tnh', xt, w1) + b1
        h = jax.nn.gelu(h, approximate=False)
        out_all = jnp.einsum('tnh,nhd->tnd', h, w2) + b2
        sel = jnp.take_along_axis(out_all, top_i[:, :, None], axis=1)
        out = (sel * top_w[:, :, None]).sum(axis=1)
        return out.reshape(orig_shape)
    x = L0_attn_x
    xn = _layernorm(x, axis=-1)
    x = x + _L0_attn_ref(xn, L0_attn_Wq, L0_attn_bq, L0_attn_Wdown, L0_attn_bdown, L0_attn_Wup, L0_attn_bup, L0_attn_Wout, L0_attn_bout) + _L0_ffn_ref(xn, L0_ffn_W_gate, L0_ffn_W_in, L0_ffn_b_in, L0_ffn_W_out, L0_ffn_b_out)
    xn = _layernorm(x, axis=-1)
    x = x + _L1_attn_ref(xn, L1_attn_W_in, L1_attn_b_in, L1_attn_k0, L1_attn_k1, L1_attn_gamma, L1_attn_beta, L1_attn_W_out, L1_attn_b_out) + _L1_ffn_ref(xn, L1_ffn_gate_w, L1_ffn_w1, L1_ffn_b1, L1_ffn_w2, L1_ffn_b2)
    return x

_drawn_inputs = setup_inputs


def setup_inputs(seed=0):
    import zlib

    import numpy as np

    out = dict(_drawn_inputs(seed))
    spreads = {'L0_attn_bq': (0.0, 0.1),
     'L0_attn_bdown': (0.0, 0.1),
     'L0_attn_bup': (0.0, 0.1),
     'L0_attn_bout': (0.0, 0.1),
     'L0_ffn_b_in': (0.0, 0.1),
     'L0_ffn_b_out': (0.0, 0.1),
     'L1_attn_b_in': (0.0, 0.8),
     'L1_attn_gamma': (1.0, 0.6),
     'L1_attn_beta': (0.0, 0.8),
     'L1_attn_b_out': (0.0, 0.8),
     'L1_ffn_b1': (0.0, 0.8),
     'L1_ffn_b2': (0.0, 0.8)}
    factors = {'L1_attn_W_in': 3.111,
     'L1_attn_k0': 3.128,
     'L1_attn_k1': 3.111,
     'L1_attn_W_out': 3.096,
     'L1_ffn_gate_w': 8.0,
     'L1_ffn_w1': 8.0,
     'L1_ffn_w2': 8.0}
    for name, (base, spread) in spreads.items():
        noise = np.random.default_rng([zlib.crc32(name.encode()), seed]).standard_normal(out[name].shape)
        drawn = base * np.exp(spread * noise) if base else spread * noise
        out[name] = jnp.asarray(drawn.astype(out[name].dtype))
    for name, factor in factors.items():
        out[name] = (out[name] * factor).astype(out[name].dtype)
    return out
```

```python
import concourse.bass as bass
from concourse import mybir
from contextlib import ExitStack

P = 128
BATCH, TIME, D = 32, 256, 128
BLKS = TIME // P
NT = BATCH * BLKS
H, DH = 16, 8
LAT = 32
E, HID = 8, 512
MK = HID // P
FT = 256
FR = FT // P
NF = 2 * NT * P // FT + E
AHEAD = 4
NFL = NF + AHEAD
TAPS = 128
SCALE = float(DH) ** -0.5
EPS = 1e-5
BIG = 3.0e38

C_ID, C_TRI, C_R8, C_THR, C_IOTA = 0, P, 2 * P, 2 * P + E, 2 * P + E + NT * P // FT
C_END = C_IOTA + NFL
NTHR = NT * P // FT
W_Q, W_G0, W_O0, W_IN1, W_G1, W_O1, W_GAM, W_BET, W_END = 0, 128, 136, 264, 648, 656, 784, 785, 786
R_BQ, R_BUP, R_BO0, R_BIN1, R_BO1, R_END = 0, 128, 384, 512, 896, 1024
WCAT = HID + MK * D + MK


def mixed_layers(nc, x, consts, w128, w32, rows, moe0, bout0, moe1, bout1, kpad0, kpad1, out):
    fp32, i32, u32 = mybir.dt.float32, mybir.dt.int32, mybir.dt.uint32
    ALU, ACT, AX = mybir.AluOpType, mybir.ActivationFunctionType, mybir.AxisListType
    ds = bass.ds

    ctx = ExitStack()
    with ctx:
        def sb(name, shape, dt=fp32):
            return ctx.enter_context(nc.sbuf_tensor(name, shape, dt))

        def sem(name):
            return ctx.enter_context(nc.semaphore(name))

        def dram(name, shape):
            return nc.dram_tensor(name, shape, fp32, kind="Internal").ap()

        sorted_x = dram("sorted_x", (NFL * FT, D))
        sorted_y = dram("sorted_y", (NF * FT, D))
        xt_d = dram("xt_d", (NT // 4, P, 4 * P))
        res_d = dram("res_d", (P, NT * D))

        X = sb("X", [P, NT, D])
        XN = sb("XN", [P, NT, D])
        BG = sb("BG", [P, 16384])
        FF = sb("FF", [P, 9232])
        cst = sb("cst", [P, C_END])
        w1s = sb("w1s", [P, W_END])
        w3s = sb("w3s", [LAT, LAT + 2 * D + P - LAT + 1])
        rws = sb("rws", [1, R_END])
        ones = sb("ones", [P, P])
        bdn = sb("bdn", [LAT, P])
        wqkv = sb("wqkv", [P, 3 * D])
        bqkv = sb("bqkv", [P, 3 * D])
        bprj = sb("bprj", [P, 3 * D])
        xg = sb("xg", [P, 2, 4 * P])
        xT = sb("xT", [P, 2, 4 * P])
        stats = sb("stats", [P, NT, 6])
        mean = sb("mean", [P, NT])
        rstd = sb("rstd", [P, NT])
        var = sb("var", [P, NT])
        tmp = sb("tmp", [P, NT])
        mhalf = sb("mhalf", [P, NT])
        wt = sb("wt", [P, 2, NT])
        small = sb("small", [P, 16, E])
        idx = sb("idx", [P, 2, NT], u32)
        eid = sb("eid", [P, NFL], i32)

        ident = cst[:, C_ID:C_ID + P]
        tri = cst[:, C_TRI:C_TRI + P]
        rank8 = cst[:, C_R8:C_R8 + E]
        thr = cst[:, C_THR:C_THR + NTHR]
        iota = cst[:, C_IOTA:C_IOTA + NFL]

        prod = BG[:, 0:8192].rearrange("p (s n) -> p s n", s=2)
        qkv = BG[:, 8192:9728].rearrange("p (s t n) -> p s t n", s=2, t=2)
        xp = BG[:, 9728:10240].rearrange("p (s n) -> p s n", s=2)
        S = BG[:, 10240:10752]
        Pr = BG[:, 10752:11264]
        O = BG[:, 11264:11520]
        On = BG[:, 11520:11776]
        OT = BG[:, 11776:12032]
        Mx = BG[:, 12032:12064]
        Sm = BG[:, 12064:12096]
        Rc = BG[:, 12096:12128]

        V = BG[:, 0:8192]
        X1 = BG[:, 8192:16384]
        X2 = X[:, :, :].rearrange("p j d -> p (j d)")
        Vj = V.rearrange("p (d j) -> p j d", j=NT)
        VX1j = BG[:, :].rearrange("p (d j) -> p j d", j=NT)
        X2j = X2.rearrange("p (d j) -> p j d", j=NT)

        wc = FF[:, 0:4112].rearrange("p (s n) -> p s n", s=4)
        bo = FF[:, 4112:4624].rearrange("p (s n) -> p s n", s=4)
        xs = FF[:, 4624:5648].rearrange("p (s n) -> p s n", s=4)
        xsT = FF[:, 5648:6160].rearrange("p (s n) -> p s n", s=2)
        hT = FF[:, 6160:8208].rearrange("p (s m n) -> p s m n", s=2, m=MK)
        ys = FF[:, 8208:9232].rearrange("p (s n) -> p s n", s=4)
        Y2 = FF[:, 0:8192].rearrange("p (j d) -> p j d", d=D)
        xTr = FF[:, 4096:5120].rearrange("p (s n) -> p s n", s=2)
        tp = FF[:, 0:4096].rearrange("p (s c n) -> p s c n", s=2, c=8)
        rt = [FF[:, i * 512:(i + 1) * 512].rearrange("p (j e) -> p j e", e=E) for i in range(9)]
        rcmp = FF[:, 5120:5120 + NFL * E]

        ps = [ctx.enter_context(nc.psum_tensor(f"ps{i}", [P, 512], fp32)) for i in range(8)]
        psH = ps[0:4]
        psT, psY, psQ, psA = ps[4:8]
        psC = [psQ, psA]

        CR = 2
        s_x = [sem(f"x_loaded{i}") for i in range(4)]
        s_cst = sem("weights_loaded")
        s_set = sem("setup_done")
        s_wps = sem("fused_weights_psum")
        s_bps = sem("bias_psum")
        s_zero = sem("zeros_ready")
        s_zf = sem("sorted_x_zeroed")
        s_v = sem("vector_step")
        s_var = sem("variance_ready")
        s_rstd = sem("rstd_ready")
        s_pw = sem("pool_step")
        s_xg = sem("xg_ready")
        s_xncp = sem("xn_copied")
        s_tr = sem("xg_transposed")
        s_xt = sem("xT_ready")
        s_gate = sem("gate_logits")
        s_xtst = [sem(f"xT_stored{i}") for i in range(2)]
        s_ex = sem("gate_exp")
        s_rin = sem("route_exp_in")
        s_tot = sem("route_totals")
        s_rank = sem("route_counts_in")
        s_route = sem("routed")
        s_sc = sem("rows_scattered")
        s_w = [sem(f"expert_tile_loaded{i}") for i in range(4)]
        s_st = [sem(f"expert_out_stored{i}") for i in range(4)]
        s_XT = sem("rows_transposed")
        s_xsT = sem("xsT_ready")
        s_H = sem("hidden_psum")
        s_gelu = sem("hidden_ready")
        s_Y = sem("expert_out_psum")
        s_yev = sem("expert_out_ready")
        s_gy = [sem(f"outputs_gathered{i}") for i in range(2)]
        s_xp = [sem(f"xp_loaded{i}") for i in range(2)]
        s_qps = sem("qkv_psum")
        s_qkv = sem("qkv_ready")
        s_pp = sem("pool_products")
        s_att = sem("attention_step")
        s_sub = sem("scores_ready")
        s_exp = sem("probs_ready")
        s_on = sem("heads_ready")
        s_ot = sem("heads_transposed")
        s_otsb = sem("headsT_ready")
        s_ao = sem("attention_out_psum")
        s_xup = sem("attention_added")
        s_comb1 = sem("first_expert_added")
        s_comb = sem("combined")
        s_vp = sem("vector_products")
        s_res = sem("residual_ready")
        s_resst = sem("residual_stored")
        s_resld = sem("residual_loaded")
        s_hg = sem("hn_ready")
        s_htr = sem("hn_transposed")
        s_hT = sem("hT_ready")
        s_pps = sem("projection_psum")
        s_pev = sem("projection_ready")
        s_tp = [sem(f"toeplitz_loaded{i}") for i in range(2)]
        s_cmm = sem("conv_psum")
        s_cev = sem("conv_ready")
        s_cg = sem("conv_gathered")
        s_ctr = sem("conv_transposed")
        s_cT = sem("convT_ready")
        s_ops = sem("conv_out_psum")
        s_oev = sem("conv_out_added")
        s_out = sem("out_stored")
        block = ctx.enter_context(nc.Block())

        B1, B2 = 7, 25
        NPAIR = NT // 2
        K_ATT = 5

        x_v = x.rearrange("b (k p) d -> p k b d", p=P)
        out_v = out.rearrange("b (k p) d -> p k b d", p=P)
        sx_v = sorted_x.rearrange("(f p r) d -> f p (r d)", p=P, r=FR)
        sy_v = sorted_y.rearrange("(f p r) d -> f p (r d)", p=P, r=FR)
        moe, bout_d, kpad = [moe0, moe1], [bout0, bout1], [kpad0, kpad1]

        def qk_product(eng, s, t):
            q = qkv[:, s, t, 0:D].rearrange("p (h e) -> p h e", h=H)
            k = qkv[:, s, t, D:3 * D].rearrange("p (g e) -> p g e", g=H)[:, :, 0:DH]
            return eng.tensor_tensor(
                prod[:, s, t * 2048:(t + 1) * 2048].rearrange("p (h g e) -> p h g e", h=H, g=H),
                q[:, :, None, :].to_broadcast([P, H, H, DH]), k[:, None, :, :].to_broadcast([P, H, H, DH]), ALU.mult)

        @block.sync
        def _(sp):
            for c in range(4):
                k, b0 = c // 2, (c % 2) * 16
                sp.dma_start(X[:, c * 16:(c + 1) * 16, :], x_v[:, k, b0:b0 + 16, :]).then_inc(s_x[c], 16)
            sp.wait_ge(s_zero, 1)
            zrow = NFL * D * FR // 4
            zv = sorted_x.rearrange("(p r) d -> p (r d)", p=P)
            for c in range(4):
                sp.dma_start(zv[:, c * zrow:(c + 1) * zrow], BG[:, 0:zrow]).then_inc(s_zf, 16)
            with sp.Fori(0, NT // 8) as u:
                for s in range(2):
                    sp.wait_ge(s_xt, 2 * u + (s + 1 + CR))
                    sp.dma_start(xt_d[ds(2 * u + s, 1), :, :].rearrange("a p n -> p (a n)"), xT[:, s, :])\
                        .then_inc(s_xtst[s], 16)
            for s in range(2):
                sp.wait_ge(s_xtst[s], 16 * (NT // 8 + 1))

            xt_pairs = xt_d.rearrange("g p (h n) -> g h p n", h=2)

            def load_xp(g, h, s):
                sp.dma_start(xp[:, s, :], xt_pairs[ds(g, 1), h, :, :].rearrange("a p n -> p (a n)"))\
                    .then_inc(s_xp[s], 16)

            def load_tile(layer, f, s):
                e = sp.value_load(eid[0:1, ds(f, 1)], min_val=0, max_val=E - 1)
                sp.dma_start(wc[:, s, :], moe[layer][ds(e, 1), :, :].rearrange("a p n -> p (a n)"))\
                    .then_inc(s_w[s], 16)
                sp.dma_start(bo[:, s, :], bout_d[layer][ds(e, 1), :].to_broadcast([P, D])).then_inc(s_w[s], 16)
                sp.dma_start(xs[:, s, :], sx_v[ds(f, 1), :, :].rearrange("a p n -> p (a n)")).then_inc(s_w[s], 16)

            def first_tiles(layer):
                sp.wait_ge(s_route, layer + 1)
                sp.wait_ge(s_sc, 16 * 2 * NT * (layer + 1))
                for f in range(AHEAD):
                    load_tile(layer, f, f)

            def next_tile(layer, v, c):
                f, s = 8 * v + c, c % 4
                sp.wait_ge(s_yev, f + (layer * NF + 1 + CR))
                sp.dma_start(sy_v[ds(f, 1), :, :].rearrange("a p n -> p (a n)"), ys[:, s, :])\
                    .then_inc(s_st[s], 16)
                load_tile(layer, f + AHEAD, s)

            load_xp(0, 0, 0)
            load_xp(0, 1, 1)

            def xp_ahead(g, h, s, done):
                sp.wait_ge(s_qps, done)
                load_xp(g, h, s)

            xp_ahead(1, 0, 0, 2)
            def half_steps(u0, n, ffn):
                with sp.Fori(u0, u0 + n) as u:
                    for i in range(2):
                        xp_ahead(u + (3 + i) // 2, (3 + i) % 2, (1 + i) % 2, 4 * u + (4 + 2 * i))
                        if ffn:
                            for c in range(4 * i, 4 * i + 4):
                                next_tile(0, u - u0, c)
            half_steps(0, 3, False)
            first_tiles(0)
            half_steps(3, 9, True)
            half_steps(12, 2, False)
            xp_ahead(15, 1, 1, 2 * 30)

            sp.wait_ge(s_res, 1)
            sp.dma_start(res_d, X2).then_inc(s_resst, 16)
            sp.wait_ge(s_route, 2)
            for cv in range(2):
                with sp.Fori(0, D // 16) as u:
                    for s in range(2):
                        sp.wait_ge(s_cmm, 2 * u + (16 * cv + s + 1))
                        src = bass.AP(kpad[cv].tensor, (2 * u + s) * (8 * 3 * TAPS) + cv,
                                      [[1, P], [3 * TAPS, 8], [1, 2 * P]])
                        sp.dma_start(tp[:, s, :, :], src).then_inc(s_tp[s], 16)
            sp.wait_ge(s_cev, 32 + CR)
            sp.wait_ge(s_resst, 16)
            sp.dma_start(X2, res_d).then_inc(s_resld, 16)
            first_tiles(1)
            with sp.Fori(0, NF // 8) as u:
                for c in range(8):
                    next_tile(1, u, c)
            for i in range(8):
                sp.wait_ge(s_comb, 9 + i)
                k, b0 = i // 4, (i % 4) * 8
                sp.dma_start(out_v[:, k, b0:b0 + 8, :], X[:, 8 * i:8 * i + 8, :]).then_inc(s_out, 16)
            sp.wait_ge(s_out, 16 * 8)
            for s in range(4):
                sp.wait_ge(s_st[s], 16 * (2 * NF // 4 + 1))

        @block.gpsimd
        def _(pool):
            pool.memset(mhalf[:, :], -0.5).then_inc(s_pw, 1)
            pool.wait_ge(s_pw, 1)
            pool.sem_inc(s_xncp, CR)

            def rstd_pow(n):
                pool.wait_ge(s_var, n)
                pool.tensor_tensor(rstd[:, :], var[:, :], mhalf[:, :], ALU.pow).then_inc(s_rstd, 1)

            def copy_xn(layer):
                with pool.Fori(0, NT // 8) as u:
                    for s in range(2):
                        pool.wait_ge(s_xg, 2 * u + (16 * layer + s + 1))
                        pool.tensor_copy(XN[:, ds(8 * u + 4 * s, 4), :].rearrange("p a d -> p (a d)"),
                                         xg[:, s, :]).then_inc(s_xncp, 1)

            def scatter(layer):
                pool.wait_ge(s_route, layer + 1)
                pool.wait_ge(s_xncp, 16 * (layer + 1) + CR)
                if layer == 0:
                    pool.wait_ge(s_zf, 64)
                else:
                    for s in range(4):
                        pool.wait_ge(s_w[s], 48 * NFL // 4)
                for j in range(NT):
                    for k in range(2):
                        pool.indirect_dma_start(
                            sorted_x, bass.IndirectOffsetOnAxis(ap=idx[:, k, j:j + 1], axis=0),
                            XN[:, j, :], None).then_inc(s_sc, 16)

            def gather(layer):
                pool.wait_ge(s_sc, 16 * 2 * NT * (layer + 1))
                for s in range(4):
                    pool.wait_ge(s_st[s], 16 * (NF // 4 * (layer + 1) + 1))
                    pool.wait_ge(s_w[s], 48 * (NFL // 4) * (layer + 1))
                for j in range(NT):
                    if j % 8 == 0 and j >= 16:
                        pool.wait_ge(s_comb, 8 * layer + j // 8 - 1)
                    for k, dst in ((0, XN), (1, Y2)):
                        pool.indirect_dma_start(
                            dst[:, j, :], None, sorted_y,
                            bass.IndirectOffsetOnAxis(ap=idx[:, k, j:j + 1], axis=0)).then_inc(s_gy[j // 8 % 2], 16)

            rstd_pow(1)
            copy_xn(0)
            scatter(0)
            for b in range(B1, B2):
                s = b % 2
                pool.wait_ge(s_qkv, 2 * b + 3)
                pool.wait_ge(s_on, b - 1)
                for t in range(2):
                    last = qk_product(pool, s, t)
                last.then_inc(s_pp, 1)
            gather(0)
            rstd_pow(2)
            copy_xn(1)
            rstd_pow(3)
            scatter(1)
            gather(1)

        @block.scalar
        def _(act):
            act.dma_start(cst[:, :], consts).then_inc(s_cst, 16)
            act.dma_start(w1s[:, :], w128).then_inc(s_cst, 16)
            act.dma_start(w3s[:, :], w32).then_inc(s_cst, 16)
            act.dma_start(rws[:, :], rows).then_inc(s_cst, 16)
            act.sem_inc(s_xt, CR)
            act.sem_inc(s_xsT, CR)
            act.sem_inc(s_gelu, CR)
            act.sem_inc(s_hT, CR)
            act.sem_inc(s_cT, CR)
            act.sem_inc(s_cg, CR)

            def copy_xT(layer):
                with act.Fori(0, NT // 8) as u:
                    for s in range(2):
                        g = 2 * u + (16 * layer + s)
                        act.wait_ge(s_tr, g + (1 + CR))
                        act.wait_ge(s_gate, g + 1)
                        if layer == 0:
                            act.wait_ge(s_xtst[s], 16 * u + 16)
                        act.copy(xT[:, s, :], psH[s][:, :]).then_inc(s_xt, 1)

            def rows_T(layer, v, c):
                s = c % 2
                F = 8 * v + (c + layer * NF)
                act.wait_ge(s_XT, F + 1)
                act.wait_ge(s_H, 2 * F + 2)
                act.copy(xsT[:, s, :], psT[:, 0:FT]).then_inc(s_xsT, 1)

            def gelus(layer, v, c):
                s = c % 2
                F = 8 * v + (c + layer * NF)
                act.wait_ge(s_Y, F + 1)
                for m in range(MK):
                    if m % 2 == 0:
                        act.wait_ge(s_H, 2 * F + (5 + m // 2))
                    g = act.activation(hT[:, s, m, :], psH[2 * s + m // 2][:, (m % 2) * FT:(m % 2 + 1) * FT],
                                       ACT.Gelu, bias=wc[:, c % 4, HID + MK * D + m:HID + MK * D + m + 1])
                g.then_inc(s_gelu, 1)

            def pair_heads(b):
                act.wait_ge(s_ot, b + 1)
                act.copy(OT, psA[:, 0:256]).then_inc(s_otsb, 1)

            def pair_exp(b):
                act.wait_ge(s_sub, b + 1)
                act.activation(Pr, S, ACT.Exp, scale=SCALE).then_inc(s_exp, 1)

            def half_steps(u0, n, ffn):
                with act.Fori(u0, u0 + n) as u:
                    if ffn:
                        rows_T(0, u - u0, 0)
                    for i in range(2):
                        b = 2 * u + (1 + i)
                        for c in range(4 * i, 4 * i + 4) if ffn else ():
                            gelus(0, u - u0, c)
                            if c < 7:
                                rows_T(0, u - u0, c + 1)
                            if c % 4 == 0:
                                pair_heads(b)
                                pair_exp(b)
                        if not ffn:
                            pair_heads(b)
                            pair_exp(b)

            copy_xT(0)
            act.wait_ge(s_rin, 1)
            act.activation(stats[:, :, 4], stats[:, :, 4], ACT.Exp).then_inc(s_ex, 1)
            pair_exp(0)
            half_steps(0, 3, False)
            half_steps(3, 9, True)
            half_steps(12, 3, False)
            pair_heads(NPAIR - 1)
            pair_exp(NPAIR - 1)
            pair_heads(NPAIR)
            copy_xT(1)
            act.wait_ge(s_rin, 2)
            lg = rt[7].rearrange("p j e -> p (j e)")
            act.activation(lg, lg, ACT.Exp).then_inc(s_ex, 1)
            with act.Fori(0, NT // 8) as u:
                for s in range(2):
                    act.wait_ge(s_htr, 2 * u + (s + 1 + CR))
                    act.wait_ge(s_pps, 8 * u + 4 * (s + 1))
                    aff = dict(scale=w1s[:, W_GAM:W_GAM + 1], bias=w1s[:, W_BET:W_BET + 1])
                    act.activation(xT[:, s, :], psH[s][:, :], ACT.Identity, **aff)
                    act.activation(xTr[:, s, :].rearrange("p (k n) -> p k n", k=4),
                                   psH[s][:, :].rearrange("p (k n) -> p k n", k=4)[:, :, ::-1],
                                   ACT.Identity, **aff).then_inc(s_hT, 1)
            act.wait_ge(s_cev, 32 + CR)
            with act.Fori(0, NT // 8) as u:
                for s in range(2):
                    act.wait_ge(s_ctr, 2 * u + (s + 1))
                    act.copy(xg[:, s, :].rearrange("p (j d) -> p j d", j=4), Vj[:, ds(8 * u + 4 * s, 4), :])\
                        .then_inc(s_cg, 1)
                    act.wait_ge(s_ctr, 2 * u + (s + 1 + CR))
                    act.wait_ge(s_ops, 2 * u + (s + 1))
                    act.copy(xT[:, s, :], psH[s][:, :]).then_inc(s_cT, 1)
            with act.Fori(0, NF // 8) as u:
                rows_T(1, u, 0)
                for c in range(8):
                    gelus(1, u, c)
                    if c < 7:
                        rows_T(1, u, c + 1)

        @block.tensor
        def _(pe):
            pe.wait_ge(s_cst, 64)
            pe.wait_ge(s_set, 1)
            pe.matmul(ps[0][:, 0:2 * D], w3s[:, 0:P], w3s[:, P:P + 2 * D], start=True, stop=True).then_inc(s_wps, 1)
            one = ones[0:1, :]
            pe.matmul(ps[1][:, 0:D], one, rws[:, R_BQ:R_BQ + D], start=True, stop=True)
            pe.matmul(ps[1][:, D:3 * D], bdn[:, :], w3s[:, P:P + 2 * D], start=True, stop=False)
            pe.matmul(ps[1][:, D:3 * D], one, rws[:, R_BUP:R_BUP + 2 * D], start=False, stop=True)
            pe.matmul(ps[2][:, 0:3 * D], one, rws[:, R_BIN1:R_BIN1 + 3 * D], start=True, stop=True).then_inc(s_bps, 1)
            pe.wait_ge(s_set, 2)
            pe.sem_inc(s_tr, CR)
            pe.sem_inc(s_gate, CR)
            pe.sem_inc(s_H, 2 * CR)
            pe.sem_inc(s_Y, CR)
            pe.sem_inc(s_ot, 1)
            pe.sem_inc(s_htr, CR)
            pe.sem_inc(s_pps, 8)
            pe.sem_inc(s_cmm, CR)
            pe.sem_inc(s_ctr, CR)
            pe.sem_inc(s_ops, CR)

            def transposes_and_gates(layer, wg):
                if layer == 1:
                    pe.wait_ge(s_xup, NPAIR + 1)
                    pe.wait_ge(s_qkv, 2 * NPAIR + 1)
                with pe.Fori(0, NT // 8) as u:
                    for s in range(2):
                        g = 2 * u + (16 * layer + s)
                        pe.wait_ge(s_xg, g + 1)
                        pe.wait_ge(s_xt, g + 1)
                        for k in range(4):
                            t = pe.transpose(psH[s][:, k * P:(k + 1) * P], xg[:, s, k * P:(k + 1) * P], ident)
                        t.then_inc(s_tr, 1)
                        pe.wait_ge(s_xt, g + (1 + CR))
                        for k in range(4):
                            t = pe.matmul(psQ[:, ds(64 * u + (32 * s + 8 * k), E)], xT[:, s, k * P:(k + 1) * P],
                                          w1s[:, wg:wg + E], start=True, stop=True)
                        t.then_inc(s_gate, 1)

            def route_counts(layer):
                pe.wait_ge(s_rank, layer + 1)
                pe.matmul(psA[:, 0:E], tri, small[:, 0, :], start=True, stop=True)
                pe.matmul(psA[:, E:2 * E], ones[:, :], small[:, 0, :], start=True, stop=True).then_inc(s_tot, 1)

            def rows_X(layer, v, c):
                F = 8 * v + (c + layer * NF)
                loads = 96 * v + 48 * (c // 4 + 1 + layer * (NFL // 4))
                pe.wait_ge(s_w[c % 4], loads)
                pe.wait_ge(s_xsT, F + CR)
                for r in range(FR):
                    t = pe.transpose(psT[:, r * P:(r + 1) * P],
                                     xs[:, c % 4, r * P:(r + 1) * P], ident)
                t.then_inc(s_XT, 1)

            def hidden(layer, v, c):
                s = c % 2
                F = 8 * v + (c + layer * NF)
                pe.wait_ge(s_xsT, F + (1 + CR))
                pe.wait_ge(s_gelu, F + 1)
                for m in range(MK):
                    t = pe.matmul(psH[2 * s + m // 2][:, (m % 2) * FT:(m % 2 + 1) * FT],
                                  wc[:, c % 4, m * P:(m + 1) * P], xsT[:, s, :], start=True, stop=True)
                    if m % 2 == 1:
                        t.then_inc(s_H, 1)

            def expert_out(layer, v, c):
                s = c % 2
                F = 8 * v + (c + layer * NF)
                pe.wait_ge(s_gelu, F + (1 + CR))
                pe.wait_ge(s_yev, F + CR)
                for r in range(FR):
                    for m in range(MK):
                        t = pe.matmul(psY[:, r * P:(r + 1) * P],
                                      hT[:, s, m, r * P:(r + 1) * P],
                                      wc[:, c % 4, HID + m * D:HID + (m + 1) * D],
                                      start=(m == 0), stop=(m == MK - 1))
                t.then_inc(s_Y, 1)

            def heads(b):
                pe.wait_ge(s_on, b)
                pe.wait_ge(s_xup, b)
                for t in range(2):
                    i = pe.transpose(psA[:, t * P:(t + 1) * P], On[:, t * P:(t + 1) * P], ident)
                i.then_inc(s_ot, 1)
                pe.wait_ge(s_otsb, b + 1)
                for t in range(2):
                    o = psA[:, 256 + t * P:256 + (t + 1) * P]
                    pe.matmul(o, one, rws[:, R_BO0:R_BO0 + D], start=True, stop=False)
                    i = pe.matmul(o, OT[:, t * P:(t + 1) * P], w1s[:, W_O0:W_O0 + D], start=False, stop=True)
                i.then_inc(s_ao, 1)

            def qkv_tile(m, s, t, loads):
                if t == 0:
                    pe.wait_ge(s_xp[s], loads)
                pe.wait_ge(s_qkv, 2 * m + (t + 1))
                pe.matmul(psQ[:, 0:3 * D], xp[:, s, t * P:(t + 1) * P], wqkv[:, :], start=True, stop=True)\
                    .then_inc(s_qps, 1)

            def half_steps(u0, n, ffn):
                with pe.Fori(u0, u0 + n) as u:
                    if ffn:
                        rows_X(0, u - u0, 0)
                    for i in range(2):
                        b = 2 * u + (1 + i)
                        m, s = b + 1, i % 2
                        loads = 16 * u + 16 * 2
                        if ffn:
                            for c in range(4 * i, 4 * i + 4):
                                hidden(0, u - u0, c)
                                if c < 7:
                                    rows_X(0, u - u0, c + 1)
                                if c > 0:
                                    expert_out(0, u - u0, c - 1)
                                if c % 4 == 0:
                                    heads(b)
                                    qkv_tile(m, s, 0, loads)
                                if c % 4 == 1:
                                    qkv_tile(m, s, 1, loads)
                        else:
                            heads(b)
                            qkv_tile(m, s, 0, loads)
                            qkv_tile(m, s, 1, loads)
                    if ffn:
                        expert_out(0, u - u0, 7)

            transposes_and_gates(0, W_G0)
            route_counts(0)
            pe.wait_ge(s_route, 1)
            for t in range(2):
                qkv_tile(0, 0, t, 16)
            for t in range(2):
                qkv_tile(1, 1, t, 16)
            half_steps(0, 3, False)
            half_steps(3, 9, True)
            half_steps(12, 3, False)
            heads(NPAIR - 1)
            heads(NPAIR)
            transposes_and_gates(1, W_G1)
            route_counts(1)
            with pe.Fori(0, NT // 8) as u:
                for s in range(2):
                    pe.wait_ge(s_hg, 2 * u + (s + 1))
                    pe.wait_ge(s_hT, 2 * u + (s + 1))
                    for k in range(4):
                        t = pe.transpose(psH[s][:, k * P:(k + 1) * P], xg[:, s, k * P:(k + 1) * P], ident)
                    t.then_inc(s_htr, 1)
                    pe.wait_ge(s_hT, 2 * u + (s + 1 + CR))
                    for k in range(4):
                        pe.wait_ge(s_pev, 8 * u + (4 * s + k + 1))
                        for q, src in ((0, xT), (1, xTr), (2, xT)):
                            t = pe.matmul(psH[2 + k % 2][:, q * D:(q + 1) * D], src[:, s, k * P:(k + 1) * P],
                                          w1s[:, W_IN1 + q * D:W_IN1 + (q + 1) * D], start=True, stop=True)
                        t.then_inc(s_pps, 1)
            pe.wait_ge(s_pev, NT + CR)
            for cv in range(2):
                diag = P if cv == 0 else 0
                with pe.Fori(0, 8) as u:
                    for s in range(2):
                        pe.wait_ge(s_tp[s], 16 * u + (16 * 8 * cv + 16))
                        pe.wait_ge(s_cev, 2 * u + (16 * cv + s + 1))
                        for k in range(8):
                            v = V[:, ds(1024 * u + (512 * s + 64 * k), NT)]
                            v0 = V[:, ds(1024 * u + (512 * s + 64 * k), NT // 2)]
                            pe.matmul(psC[s][:, k * NT:(k + 1) * NT], tp[:, s, k, diag:diag + P], v, start=True, stop=False)
                            t = pe.matmul(psC[s][:, k * NT + NT // 2:(k + 1) * NT], tp[:, s, k, P - diag:2 * P - diag], v0,
                                          start=False, stop=True)
                        t.then_inc(s_cmm, 1)
            with pe.Fori(0, NT // 8) as u:
                for s in range(2):
                    pe.wait_ge(s_cg, 2 * u + (s + 1 + CR))
                    pe.wait_ge(s_cT, 2 * u + (s + 1))
                    for k in range(4):
                        t = pe.transpose(psH[s][:, k * P:(k + 1) * P], xg[:, s, k * P:(k + 1) * P], ident)
                    t.then_inc(s_ctr, 1)
                    pe.wait_ge(s_cT, 2 * u + (s + 1 + CR))
                    pe.wait_ge(s_oev, 2 * u + (s + 1))
                    for k in range(4):
                        o = psH[2 + s][:, k * P:(k + 1) * P]
                        pe.matmul(o, one, rws[:, R_BO1:R_BO1 + D], start=True, stop=False)
                        t = pe.matmul(o, xT[:, s, k * P:(k + 1) * P], w1s[:, W_O1:W_O1 + D], start=False, stop=True)
                    t.then_inc(s_ops, 1)
            pe.wait_ge(s_oev, 16 + CR)
            with pe.Fori(0, NF // 8) as u:
                rows_X(1, u, 0)
                for c in range(8):
                    hidden(1, u, c)
                    if c < 7:
                        rows_X(1, u, c + 1)
                    if c > 0:
                        expert_out(1, u, c - 1)
                expert_out(1, u, 7)

        @block.vector
        def _(dve):
            steps = [0]

            def link(ins):
                steps[0] += 1
                ins.then_inc(s_v, 1)
                dve.wait_ge(s_v, steps[0])

            zrow = NFL * D * FR // 4
            dve.memset(BG[:, 0:zrow], 0.0).then_inc(s_zero, 1)
            dve.memset(ones[:, :], 1.0)
            dve.wait_ge(s_cst, 64)
            dve.tensor_copy(bdn[:, :], w3s[:, P + 2 * D:P + 2 * D + 1].to_broadcast([LAT, P])).then_inc(s_set, 1)
            dve.sem_inc(s_yev, CR)
            dve.sem_inc(s_pev, CR)
            dve.sem_inc(s_cev, CR)
            dve.sem_inc(s_oev, CR)
            dve.sem_inc(s_xup, 1)
            dve.sem_inc(s_otsb, 1)
            dve.sem_inc(s_qkv, 1)
            for s in range(4):
                dve.sem_inc(s_st[s], 16)
            for s in range(2):
                dve.sem_inc(s_xtst[s], 16)
            dve.wait_ge(s_wps, 1)
            dve.tensor_copy(wqkv[:, 0:D], w1s[:, W_Q:W_Q + D])
            dve.tensor_copy(wqkv[:, D:3 * D], ps[0][:, 0:2 * D])
            dve.wait_ge(s_bps, 1)
            dve.tensor_copy(bqkv[:, :], ps[1][:, 0:3 * D])
            dve.tensor_copy(bprj[:, :], ps[2][:, 0:3 * D]).then_inc(s_set, 1)

            def norm_stats(src):
                with dve.Fori(0, NT // 4) as u:
                    for k in range(4):
                        dve.bn_stats(stats[:, ds(4 * u + k, 1), :].rearrange("p a n -> p (a n)"),
                                     src[:, ds(4 * u + k, 1), :].rearrange("p a n -> p (a n)"))
                link(dve.memset(tmp[:, 0:1], 0.0))
                me, qe, mo, qo = (stats[:, :, i] for i in (1, 2, 4, 5))
                dve.tensor_tensor(mean[:, :], me, mo, ALU.add)
                link(dve.tensor_tensor(tmp[:, :], me, mo, ALU.subtract))
                dve.tensor_tensor(var[:, :], qe, qo, ALU.add)
                link(dve.tensor_tensor(tmp[:, :], tmp[:, :], tmp[:, :], ALU.mult))
                dve.tensor_scalar(mean[:, :], mean[:, :], 0.5, None, ALU.mult)
                link(dve.tensor_scalar(tmp[:, :], tmp[:, :], 0.25, EPS, ALU.mult, ALU.add))
                dve.scalar_tensor_tensor(out=var[:, :], in0=var[:, :], scalar=1.0 / D, in1=tmp[:, :],
                                         op0=ALU.mult, op1=ALU.add).then_inc(s_var, 1)

            def normalise(src, u, s, done):
                for k in range(4):
                    j = 8 * u + (4 * s + k)
                    t = dve.tensor_scalar(xg[:, s, k * D:(k + 1) * D],
                                          src[:, ds(j, 1), :].rearrange("p a n -> p (a n)"),
                                          mean[:, ds(j, 1)], rstd[:, ds(j, 1)], ALU.subtract, ALU.mult)
                t.then_inc(done, 1)

            def norm_and_transpose(layer):
                norm_stats(X)
                dve.wait_ge(s_rstd, layer + 1)
                with dve.Fori(0, NT // 8) as u:
                    for s in range(2):
                        g = 2 * u + (16 * layer + s)
                        dve.wait_ge(s_tr, g + 1)
                        dve.wait_ge(s_xncp, g + 1)
                        normalise(X, u, s, s_xg)

            def b3(ap, n):
                return ap[:, :, None].to_broadcast([P, NT, n])

            def be(ap):
                return ap[:, None, :].to_broadcast([P, NT, E])

            def route(layer):
                dve.wait_ge(s_gate, 16 * (layer + 1) + CR)
                L, oh1, oh2, t0, t1, Mk, C, L0 = rt[0:8]
                lg = psQ[:, :].rearrange("p (j e) -> p j e", e=E)
                m1, m2, k1, k2, ta, tb = (stats[:, :, i] for i in range(6))
                if layer == 0:
                    link(dve.tensor_copy(L, lg))
                else:
                    link(dve.tensor_copy(L0, lg))
                    link(dve.tensor_reduce(m1, L0, AX.X, ALU.max))
                    link(dve.tensor_tensor(L0, L0, b3(m1, E), ALU.subtract))
                    dve.sem_inc(s_rin, 1)
                    dve.wait_ge(s_ex, 2)
                    link(dve.tensor_reduce(m1, L0, AX.X, ALU.add))
                    link(dve.reciprocal(m2, m1))
                    link(dve.tensor_tensor(L, L0, b3(m2, E), ALU.mult))
                for m, k, oh in ((m1, k1, oh1), (m2, k2, oh2)):
                    link(dve.tensor_reduce(m, L, AX.X, ALU.max))
                    link(dve.tensor_tensor(t0, L, b3(m, E), ALU.is_equal))
                    link(dve.tensor_tensor(t0, t0, be(rank8), ALU.mult))
                    link(dve.tensor_reduce(k, t0, AX.X, ALU.max))
                    link(dve.tensor_tensor(oh, be(rank8), b3(k, E), ALU.is_equal))
                    if m is m1:
                        link(dve.tensor_scalar(t1, oh, BIG, None, ALU.mult))
                        link(dve.tensor_tensor(L, L, t1, ALU.subtract))
                if layer == 0:
                    link(dve.tensor_tensor(ta, m2, m1, ALU.subtract))
                    dve.sem_inc(s_rin, 1)
                    dve.wait_ge(s_ex, 1)
                    link(dve.tensor_scalar(tb, ta, 1.0, None, ALU.add))
                    link(dve.reciprocal(wt[:, 0, :], tb))
                    link(dve.tensor_tensor(wt[:, 1, :], ta, wt[:, 0, :], ALU.mult))
                else:
                    link(dve.tensor_tensor(ta, m1, m2, ALU.add))
                    link(dve.tensor_scalar(ta, ta, 1e-9, None, ALU.add))
                    link(dve.reciprocal(tb, ta))
                    dve.tensor_tensor(wt[:, 0, :], m1, tb, ALU.mult)
                    link(dve.tensor_tensor(wt[:, 1, :], m2, tb, ALU.mult))
                link(dve.tensor_tensor(Mk, oh1, oh2, ALU.add))
                for e in range(E):
                    sc = dve.tensor_tensor_scan(C[:, :, e], ones[:, 0:NT], Mk[:, :, e], 0.0, ALU.mult, ALU.add)
                link(sc)
                dve.tensor_copy(small[:, 0, :], C[:, NT - 1, :]).then_inc(s_rank, 1)
                dve.wait_ge(s_tot, layer + 1)
                link(dve.tensor_copy(small[:, 1:3, :].rearrange("p a e -> p (a e)"), psA[:, 0:2 * E]))
                base, tot, nt, end, off = (small[:, i, :] for i in range(1, 6))
                cmp = rcmp[:, 0:E * NTHR].rearrange("p (e q) -> p e q", e=E)
                link(dve.tensor_tensor(cmp, tot[:, :, None].to_broadcast([P, E, NTHR]),
                                       thr[:, None, :].to_broadcast([P, E, NTHR]), ALU.is_gt))
                link(dve.tensor_reduce(nt, cmp, AX.X, ALU.add))
                link(dve.tensor_tensor_scan(end, ones[:, 0:E], nt, 0.0, ALU.mult, ALU.add))
                link(dve.tensor_tensor(off, end, nt, ALU.subtract))
                link(dve.tensor_scalar(off, off, float(FT), -1.0, ALU.mult, ALU.add))
                link(dve.tensor_tensor(off, off, base, ALU.add))
                link(dve.tensor_tensor(C, C, be(off), ALU.add))
                for k, oh in ((0, oh1), (1, oh2)):
                    link(dve.tensor_tensor(t0, C, oh, ALU.mult))
                    link(dve.tensor_reduce(ta, t0, AX.X, ALU.add))
                    link(dve.tensor_copy(idx[:, k, :], ta))
                ecmp = rcmp[:, 0:NFL * E].rearrange("p (f e) -> p f e", e=E)
                link(dve.tensor_tensor(ecmp, iota[:, :, None].to_broadcast([P, NFL, E]),
                                       end[:, None, :].to_broadcast([P, NFL, E]), ALU.is_ge))
                link(dve.tensor_reduce(L.rearrange("p j e -> p (j e)")[:, 0:NFL], ecmp, AX.X, ALU.add))
                dve.tensor_scalar(eid[:, :], L.rearrange("p j e -> p (j e)")[:, 0:NFL], float(E - 1), None,
                                  ALU.min).then_inc(s_route, 1)

            def expert_evac(layer, v, c):
                F = 8 * v + (c + layer * NF)
                stored = 32 * v + 16 * (c // 4 + layer * (NF // 4) + 1)
                dve.wait_ge(s_Y, F + (1 + CR))
                dve.wait_ge(s_st[c % 4], stored)
                s = c % 2
                dve.tensor_tensor(ys[:, c % 4, :].rearrange("p (r d) -> p r d", r=FR),
                                  psY[:, 0:FT].rearrange("p (r d) -> p r d", r=FR),
                                  bo[:, c % 4, :][:, None, :].to_broadcast([P, FR, D]), ALU.add)\
                    .then_inc(s_yev, 1)

            def evac_qkv(m, s, t):
                dve.wait_ge(s_qps, 2 * m + (t + 1))
                dve.tensor_tensor(qkv[:, s, t, :], psQ[:, 0:3 * D], bqkv[:, :], ALU.add).then_inc(s_qkv, 1)

            def add_heads(b):
                dve.wait_ge(s_ao, b)
                xv = X[:, ds(2 * b - 2, 2), :].rearrange("p a d -> p (a d)")
                dve.tensor_tensor(xv, xv, psA[:, 256:512], ALU.add).then_inc(s_xup, 1)

            def combine(layer, i, par, gathered):
                dve.wait_ge(s_gy[par], gathered)
                for k, src in ((0, XN), (1, Y2)):
                    for c in range(8):
                        j = 8 * i + c
                        xv = X[:, ds(j, 1), :].rearrange("p a d -> p (a d)")
                        t = dve.scalar_tensor_tensor(
                            out=xv, in0=src[:, ds(j, 1), :].rearrange("p a d -> p (a d)"),
                            scalar=wt[:, k, ds(j, 1)], in1=xv, op0=ALU.mult, op1=ALU.add)
                    t.then_inc(s_comb1 if k == 0 else s_comb, 1)
                    dve.wait_ge(s_comb1 if k == 0 else s_comb, i + (8 * layer + 1))

            def pair(b, s, skipped=0, on_pool=False, evacs=(), first=False, last=False, combines=None):
                def step(n, ins):
                    ins.then_inc(s_att, 1)
                    dve.wait_ge(s_att, K_ATT * b + n)

                def evac(n):
                    if evacs:
                        expert_evac(0, *evacs[n])

                if on_pool:
                    dve.wait_ge(s_pp, b - (B1 - 1))
                else:
                    dve.wait_ge(s_qkv, 2 * b + 3)
                    for t in range(2):
                        i = qk_product(dve, s, t)
                    i.then_inc(s_vp, 1)
                    dve.wait_ge(s_vp, b + (1 - skipped))
                step(1, dve.tensor_reduce(S, prod[:, s, :].rearrange("p (n d) -> p n d", d=DH), AX.X, ALU.add))
                S3 = S.rearrange("p (n g) -> p n g", g=H)
                step(2, dve.tensor_reduce(Mx, S3, AX.X, ALU.max))
                dve.tensor_tensor(S3, S3, Mx[:, :, None].to_broadcast([P, 2 * H, H]), ALU.subtract).then_inc(s_sub, 1)
                if not first:
                    add_heads(b)
                if not last:
                    evac_qkv(b + 1, 1 - s, 0)
                    evac(0)
                    evac_qkv(b + 1, 1 - s, 1)
                dve.wait_ge(s_exp, b + 1)
                P3 = Pr.rearrange("p (n g) -> p n g", g=H)
                step(3, dve.tensor_reduce(Sm, P3, AX.X, ALU.add))
                dve.reciprocal(Rc, Sm)
                evac(1)
                for t in range(2):
                    kv = qkv[:, s, t, D:3 * D].rearrange("p (g e) -> p g e", g=H)
                    v = kv[:, :, DH:2 * DH].rearrange("p g e -> p e g")
                    i = dve.tensor_tensor(
                        prod[:, s, t * 2048:(t + 1) * 2048].rearrange("p (h e g) -> p h e g", h=H, e=DH),
                        Pr[:, t * 256:(t + 1) * 256].rearrange("p (h g) -> p h g", h=H)[:, :, None, :]
                        .to_broadcast([P, H, DH, H]),
                        v[:, None, :, :].to_broadcast([P, H, DH, H]), ALU.mult)
                step(4, i)
                evac(2)
                step(5, dve.tensor_reduce(O, prod[:, s, :].rearrange("p (n g) -> p n g", g=H), AX.X, ALU.add))
                evac(3)
                dve.wait_ge(s_ot, b + 1)
                dve.tensor_tensor(On.rearrange("p (n e) -> p n e", e=DH), O.rearrange("p (n e) -> p n e", e=DH),
                                  Rc[:, :, None].to_broadcast([P, 2 * H, DH]), ALU.mult).then_inc(s_on, 1)
                if combines is not None:
                    combine(0, *combines)

            def half_steps(u0, n, ffn, comb=False):
                with dve.Fori(u0, u0 + n) as u:
                    for i in range(2):
                        evs = [(u - u0, 4 * i + c) for c in range(4)] if ffn else ()
                        pair(2 * u + (1 + i), (1 + i) % 2, B2 - B1 if comb else 0, on_pool=ffn, evacs=evs,
                             combines=(2 * u + (i - 2 * u0), i, 256 * u + 256 * (1 - u0)) if comb else None)

            for c in range(4):
                dve.wait_ge(s_x[c], 16)
            norm_and_transpose(0)
            route(0)
            dve.wait_ge(s_zf, 64)
            evac_qkv(0, 0, 0)
            evac_qkv(0, 0, 1)
            pair(0, 0, first=True)
            half_steps(0, 3, False)
            half_steps(3, 9, True)
            half_steps(12, 3, False, comb=True)
            pair(NPAIR - 1, 1, B2 - B1, last=True, combines=(6, 0, 256 * 4))
            add_heads(NPAIR)
            dve.wait_ge(s_xup, NPAIR + 1)
            combine(0, 7, 1, 256 * 4)

            norm_and_transpose(1)
            dve.wait_ge(s_xncp, 32 + CR)
            norm_stats(XN)
            route(1)
            dve.tensor_tensor(X2, X2, XN[:, :, :].rearrange("p j d -> p (j d)"), ALU.add).then_inc(s_res, 1)
            dve.wait_ge(s_rstd, 3)
            with dve.Fori(0, NT // 8) as u:
                for s in range(2):
                    dve.wait_ge(s_htr, 2 * u + (s + 1))
                    normalise(XN, u, s, s_hg)
                    for k in range(4):
                        j = 8 * u + (4 * s + k)
                        bank = psH[2 + k % 2]
                        if k == 0 and s == 0:
                            dve.wait_ge(s_resst, 16)
                        dve.wait_ge(s_pps, j + (1 + 8))
                        dve.tensor_tensor(VX1j[:, ds(j, 1), :].rearrange("p a d -> p (a d)"), bank[:, 0:2 * D],
                                          bprj[:, 0:2 * D], ALU.add)
                        dve.tensor_tensor(X2j[:, ds(j, 1), :].rearrange("p a d -> p (a d)"), bank[:, 2 * D:3 * D],
                                          bprj[:, 2 * D:3 * D], ALU.add).then_inc(s_pev, 1)
            for cv, gate in ((0, X1), (1, X2)):
                with dve.Fori(0, 8) as u:
                    for s in range(2):
                        dve.wait_ge(s_cmm, 2 * u + (16 * cv + s + 1 + CR))
                        sl = ds(1024 * u + 512 * s, 512)
                        dve.tensor_tensor(V[:, sl], psC[s][:, :], gate[:, sl], ALU.mult).then_inc(s_cev, 1)
            dve.wait_ge(s_resld, 16)
            with dve.Fori(0, NT // 8) as u:
                for s in range(2):
                    dve.wait_ge(s_ops, 2 * u + (s + 1 + CR))
                    xv = X[:, ds(8 * u + 4 * s, 4), :].rearrange("p a d -> p (a d)")
                    dve.tensor_tensor(xv, xv, psH[2 + s][:, :], ALU.add).then_inc(s_oev, 1)
            with dve.Fori(0, NF // 8) as u:
                for c in range(8):
                    expert_evac(1, u, c)
            dve.wait_ge(s_oev, 16 + CR)
            for i in range(8):
                combine(1, i, i % 2, 256 * (i // 2 + 5))


def kernel(**inputs):
    import numpy as _np
    import concourse.bacc as _bacc
    from concourse import mybir as _mybir
    from concourse.bass_utils import run_bass_kernel_spmd as _run

    a = {k: _np.asarray(v) for k, v in inputs.items()}
    consts = _np.concatenate([
        _np.eye(P), _np.triu(_np.ones((P, P)), 1), _np.tile(_np.arange(E, 0, -1), (P, 1)),
        _np.tile(FT * _np.arange(NTHR), (P, 1)), _np.tile(_np.arange(NFL), (P, 1))], 1).astype(_np.float32)

    def experts(w_in, b_in, w_out):
        return _np.concatenate([w_in, w_out.reshape(E, MK, P, D).transpose(0, 2, 1, 3).reshape(E, P, MK * D),
                                b_in.reshape(E, MK, P).transpose(0, 2, 1)], 2)

    def padded(k):
        return _np.pad(k, ((0, 0), (TAPS, TAPS)))

    arrays = {
        "x": a["L0_attn_x"],
        "consts": consts,
        "w128": _np.concatenate([a["L0_attn_Wq"], a["L0_ffn_W_gate"], a["L0_attn_Wout"], a["L1_attn_W_in"],
                                 a["L1_ffn_gate_w"].T, a["L1_attn_W_out"], a["L1_attn_gamma"][:, None],
                                 a["L1_attn_beta"][:, None]], 1),
        "w32": _np.concatenate([a["L0_attn_Wdown"].T, a["L0_attn_Wup"], a["L0_attn_bdown"][:, None]], 1),
        "rows": _np.concatenate([a["L0_attn_bq"], a["L0_attn_bup"], a["L0_attn_bout"], a["L1_attn_b_in"],
                                 a["L1_attn_b_out"]])[None, :],
        "moe0": experts(a["L0_ffn_W_in"], a["L0_ffn_b_in"], a["L0_ffn_W_out"]),
        "bout0": a["L0_ffn_b_out"],
        "moe1": experts(a["L1_ffn_w1"], a["L1_ffn_b1"], a["L1_ffn_w2"]),
        "bout1": a["L1_ffn_b2"],
        "kpad0": padded(a["L1_attn_k0"][0, :, ::-1]),
        "kpad1": padded(a["L1_attn_k1"][0]),
    }
    nc = _bacc.Bacc("TRN2", target_bir_lowering=False, num_devices=1)
    arrays = {f"in_{k}": _np.ascontiguousarray(v) for k, v in arrays.items()}
    args = [nc.dram_tensor(k, v.shape, _mybir.dt.from_np(v.dtype), kind="ExternalInput").ap()
            for k, v in arrays.items()]
    out = nc.dram_tensor("out_0", (BATCH, TIME, D), _mybir.dt.float32, kind="ExternalOutput").ap()
    mixed_layers(nc, *args, out)
    return _run(nc, [arrays], core_ids=[0]).results[0]["out_0"]
```

```python
import concourse.bass as bass
from concourse import mybir
from contextlib import ExitStack

P = 128
BATCH, TIME, D = 32, 256, 128
BLKS = TIME // P
NT = BATCH * BLKS
H, DH = 16, 8
LAT = 32
E, HID = 8, 512
MK = HID // P
FT = 256
FR = FT // P
NF = 2 * NT * P // FT + E
AHEAD = 4
NFL = NF + AHEAD
TAPS = 128
SCALE = float(DH) ** -0.5
EPS = 1e-5
BIG = 3.0e38

C_ID, C_TRI, C_R8, C_THR, C_IOTA = 0, P, 2 * P, 2 * P + E, 2 * P + E + NT * P // FT
C_M1 = C_IOTA + NFL
C_M2 = C_M1 + 1
C_END = C_M2 + 1
NTHR = NT * P // FT
W_Q, W_G0, W_O0, W_IN1, W_G1, W_O1, W_GAM, W_BET, W_END = 0, 128, 136, 264, 648, 656, 784, 785, 786
R_BQ, R_BUP, R_BO0, R_BIN1, R_BO1, R_END = 0, 128, 384, 512, 896, 1024
WCAT = HID + MK * D + MK


def mixed_layers(nc, x, consts, w128, w32, rows, moe0, bout0, moe1, bout1, kpad0, kpad1, out):
    fp32, bf16, i32, u32 = mybir.dt.float32, mybir.dt.bfloat16, mybir.dt.int32, mybir.dt.uint32
    ALU, ACT, AX = mybir.AluOpType, mybir.ActivationFunctionType, mybir.AxisListType
    ds = bass.ds

    ctx = ExitStack()
    with ctx:
        def sb(name, shape, dt=fp32):
            return ctx.enter_context(nc.sbuf_tensor(name, shape, dt))

        def sem(name):
            return ctx.enter_context(nc.semaphore(name))

        def dram(name, shape, dt=fp32):
            return nc.dram_tensor(name, shape, dt, kind="Internal").ap()

        sorted_x = dram("sorted_x", (NFL * FT, D))
        sorted_y = dram("sorted_y", (NF * FT, D))
        xt_d = dram("xt_d", (NT // 4, P, 4 * P))
        bo3_d = [dram(f"bo3_{n}", (3, E * D), bf16) for n in range(2)]
        res_d = dram("res_d", (P, NT * D))

        X = sb("X", [P, NT, D])
        XN = sb("XN", [P, NT, D])
        BG = sb("BG", [P, 16384])
        FF = sb("FF", [P, 9232])
        cst = sb("cst", [P, C_END])
        w1s = sb("w1s", [P, W_END])
        w3s = sb("w3s", [LAT, LAT + 2 * D + P - LAT + 1])
        rws = sb("rws", [1, R_END])
        ones = sb("ones", [P, P])
        bdn = sb("bdn", [LAT, P])
        wqkv = sb("wqkv", [P, 3 * D])
        brow = sb("brow", [3, 5 * D])
        b3 = sb("b3", [3, 5 * D], bf16)
        ones3 = sb("ones3", [3, P], bf16)
        bprj = sb("bprj", [P, 3 * D])
        xg = sb("xg", [P, 2, 4 * P])
        xT = sb("xT", [P, 2, 4 * P])
        stats = sb("stats", [P, NT, 6])
        mean = sb("mean", [P, NT])
        rstd = sb("rstd", [P, NT])
        var = sb("var", [P, NT])
        tmp = sb("tmp", [P, NT])
        sdev = sb("sdev", [P, NT])
        wt = sb("wt", [P, 2, NT])
        small = sb("small", [P, 16, E])
        idx = sb("idx", [P, 2, NT], u32)
        eid = sb("eid", [P, NFL], i32)

        ident = cst[:, C_ID:C_ID + P]
        tri = cst[:, C_TRI:C_TRI + P]
        rank8 = cst[:, C_R8:C_R8 + E]
        thr = cst[:, C_THR:C_THR + NTHR]
        iota = cst[:, C_IOTA:C_IOTA + NFL]

        prod = BG[:, 0:8192].rearrange("p (s n) -> p s n", s=2)
        qkv = BG[:, 8192:9728].rearrange("p (s t n) -> p s t n", s=2, t=2)
        xp = BG[:, 9728:10240].rearrange("p (s n) -> p s n", s=2)
        S = BG[:, 10240:10752]
        Pr = BG[:, 10752:11264]
        O = BG[:, 11264:11520]
        On = BG[:, 11520:11776]
        OT = BG[:, 11776:12032]
        Mx = BG[:, 12032:12064]
        Sm = BG[:, 12064:12096]
        Rc = BG[:, 12096:12128]

        V = BG[:, 0:8192]
        X1 = BG[:, 8192:16384]
        X2 = X[:, :, :].rearrange("p j d -> p (j d)")
        Vj = V.rearrange("p (d j) -> p j d", j=NT)
        VX1j = BG[:, :].rearrange("p (d j) -> p j d", j=NT)
        X2j = X2.rearrange("p (d j) -> p j d", j=NT)

        wc = FF[:, 0:4112].rearrange("p (s n) -> p s n", s=4)
        bo = FF[0:3, 4112:4368].bitcast(bf16).rearrange("p (s n) -> p s n", s=4)
        xs = FF[:, 4624:5648].rearrange("p (s n) -> p s n", s=4)
        xsT = FF[:, 5648:6160].rearrange("p (s n) -> p s n", s=2)
        hT = FF[:, 6160:8208].rearrange("p (s m n) -> p s m n", s=2, m=MK)
        ys = FF[:, 8208:9232].rearrange("p (s n) -> p s n", s=4)
        Y2 = FF[:, 0:2048].rearrange("p (j d) -> p j d", d=D)
        tp = FF[:, 2048:6144].rearrange("p (s c n) -> p s c n", s=2, c=8)
        xTr = FF[:, 6160:7184].rearrange("p (s n) -> p s n", s=2)
        boutf = FF[0:3, 0:2048].rearrange("p (l n) -> p l n", l=2)
        part = FF[0:3, 2048:3072]
        partb = FF[0:3, 3072:3584].bitcast(bf16)
        bout3 = FF[0:3, 3584:4608].bitcast(bf16).rearrange("p (l n) -> p l n", l=2)
        rt = [FF[:, i * 512:(i + 1) * 512].rearrange("p (j e) -> p j e", e=E) for i in range(9)]
        rcmp = FF[:, 5120:5120 + NFL * E]

        ps = [ctx.enter_context(nc.psum_tensor(f"ps{i}", [P, 512], fp32)) for i in range(8)]
        psH = ps[0:4]
        psT, psY, psQ, psA = ps[4:8]
        psC = [psQ, psA]

        CR = 2
        s_x = [sem(f"x_loaded{i}") for i in range(4)]
        s_cst = sem("weights_loaded")
        s_set = sem("setup_done")
        s_wps = sem("fused_weights_psum")
        s_bps = sem("bias_psum")
        s_zero = sem("zeros_ready")
        s_zf = sem("sorted_x_zeroed")
        s_v = sem("vector_step")
        s_var = sem("variance_ready")
        s_rstd = sem("rstd_ready")
        s_bf = sem("bout_loaded")
        s_bo3 = sem("bout_split")
        s_bo3st = sem("bout_parts_stored")
        s_xg = sem("xg_ready")
        s_xncp = sem("xn_copied")
        s_tr = sem("xg_transposed")
        s_xt = sem("xT_ready")
        s_gate = sem("gate_logits")
        s_xtst = [sem(f"xT_stored{i}") for i in range(2)]
        s_ex = sem("gate_exp")
        s_rin = sem("route_exp_in")
        s_tot = sem("route_totals")
        s_rank = sem("route_counts_in")
        s_route = sem("routed")
        s_sc = sem("rows_scattered")
        s_w = [sem(f"expert_tile_loaded{i}") for i in range(4)]
        s_st = [sem(f"expert_out_stored{i}") for i in range(4)]
        s_XT = sem("rows_transposed")
        s_xsT = sem("xsT_ready")
        s_H = sem("hidden_psum")
        s_gelu = sem("hidden_ready")
        s_Y = sem("expert_out_psum")
        s_yev = sem("expert_out_ready")
        s_gy = [sem(f"outputs_gathered{i}") for i in range(2)]
        s_xp = [sem(f"xp_loaded{i}") for i in range(2)]
        s_qps = sem("qkv_psum")
        s_qkv = sem("qkv_ready")
        s_pp = sem("pool_products")
        s_att = sem("attention_step")
        s_sub = sem("scores_ready")
        s_exp = sem("probs_ready")
        s_on = sem("heads_ready")
        s_ot = sem("heads_transposed")
        s_otsb = sem("headsT_ready")
        s_ao = sem("attention_out_psum")
        s_xup = sem("attention_added")
        s_comb1 = sem("first_expert_added")
        s_comb = sem("combined")
        s_vp = sem("vector_products")
        s_res = sem("residual_ready")
        s_resst = sem("residual_stored")
        s_resld = sem("residual_loaded")
        s_hg = sem("hn_ready")
        s_htr = sem("hn_transposed")
        s_hT = sem("hT_ready")
        s_pps = sem("projection_psum")
        s_pev = sem("projection_ready")
        s_tp = [sem(f"toeplitz_loaded{i}") for i in range(2)]
        s_cmm = sem("conv_psum")
        s_cev = sem("conv_ready")
        s_cg = sem("conv_gathered")
        s_ctr = sem("conv_transposed")
        s_cT = sem("convT_ready")
        s_ops = sem("conv_out_psum")
        s_oev = sem("conv_out_added")
        s_fin = sem("tiles_final")
        s_out = sem("out_stored")
        block = ctx.enter_context(nc.Block())

        B1, B2 = 7, 25
        NPAIR = NT // 2
        K_ATT = 5

        x_v = x.rearrange("b (k p) d -> p k b d", p=P)
        out_v = out.rearrange("b (k p) d -> p k b d", p=P)
        sx_v = sorted_x.rearrange("(f p r) d -> f p (r d)", p=P, r=FR)
        sy_v = sorted_y.rearrange("(f p r) d -> f p (r d)", p=P, r=FR)
        moe, bout_d, kpad = [moe0, moe1], [bout0, bout1], [kpad0, kpad1]

        def qk_product(eng, s, t):
            q = qkv[:, s, t, 0:D].rearrange("p (h e) -> p h e", h=H)
            k = qkv[:, s, t, D:3 * D].rearrange("p (g e) -> p g e", g=H)[:, :, 0:DH]
            return eng.tensor_tensor(
                prod[:, s, t * 2048:(t + 1) * 2048].rearrange("p (h g e) -> p h g e", h=H, g=H),
                q[:, :, None, :].to_broadcast([P, H, H, DH]), k[:, None, :, :].to_broadcast([P, H, H, DH]), ALU.mult)

        @block.sync
        def _(sp):
            for c in range(4):
                k, b0 = c // 2, (c % 2) * 16
                sp.dma_start(X[:, c * 16:(c + 1) * 16, :], x_v[:, k, b0:b0 + 16, :]).then_inc(s_x[c], 16)
            for layer in range(2):
                sp.dma_start(boutf[:, layer, :], bout_d[layer].rearrange("(a e) d -> a (e d)", a=1)
                             .to_broadcast([3, E * D])).then_inc(s_bf, 16)
            sp.wait_ge(s_zero, 1)
            zrow = NFL * D * FR // 4
            zv = sorted_x.rearrange("(p r) d -> p (r d)", p=P)
            for c in range(4):
                sp.dma_start(zv[:, c * zrow:(c + 1) * zrow], BG[:, 0:zrow]).then_inc(s_zf, 16)
            with sp.Fori(0, NT // 8) as u:
                for s in range(2):
                    sp.wait_ge(s_xt, 2 * u + (s + 1 + CR))
                    sp.dma_start(xt_d[ds(2 * u + s, 1), :, :].rearrange("a p n -> p (a n)"), xT[:, s, :])\
                        .then_inc(s_xtst[s], 16)
            for s in range(2):
                sp.wait_ge(s_xtst[s], 16 * (NT // 8 + 1))
            sp.wait_ge(s_bo3, 1)
            for layer in range(2):
                sp.dma_start(bo3_d[layer], bout3[:, layer, :]).then_inc(s_bo3st, 16)
            sp.wait_ge(s_bo3st, 32)

            xt_pairs = xt_d.rearrange("g p (h n) -> g h p n", h=2)

            def load_xp(g, h, s):
                sp.dma_start(xp[:, s, :], xt_pairs[ds(g, 1), h, :, :].rearrange("a p n -> p (a n)"))\
                    .then_inc(s_xp[s], 16)

            def load_tile(layer, f, s):
                e = sp.value_load(eid[0:1, ds(f, 1)], min_val=0, max_val=E - 1)
                sp.dma_start(wc[:, s, :], moe[layer][ds(e, 1), :, :].rearrange("a p n -> p (a n)"))\
                    .then_inc(s_w[s], 16)
                sp.dma_start(bo[:, s, :], bo3_d[layer][:, ds(e * D, D)]).then_inc(s_w[s], 16)
                sp.dma_start(xs[:, s, :], sx_v[ds(f, 1), :, :].rearrange("a p n -> p (a n)")).then_inc(s_w[s], 16)

            def first_tiles(layer):
                sp.wait_ge(s_route, layer + 1)
                sp.wait_ge(s_sc, 16 * 2 * NT * (layer + 1))
                for f in range(AHEAD):
                    load_tile(layer, f, f)

            def next_tile(layer, v, c):
                f, s = 8 * v + c, c % 4
                sp.wait_ge(s_yev, f + (layer * NF + 1 + CR))
                sp.dma_start(sy_v[ds(f, 1), :, :].rearrange("a p n -> p (a n)"), ys[:, s, :])\
                    .then_inc(s_st[s], 16)
                load_tile(layer, f + AHEAD, s)

            load_xp(0, 0, 0)
            load_xp(0, 1, 1)

            def xp_ahead(g, h, s, done):
                sp.wait_ge(s_qps, done)
                load_xp(g, h, s)

            xp_ahead(1, 0, 0, 2)
            def half_steps(u0, n, ffn):
                with sp.Fori(u0, u0 + n) as u:
                    for i in range(2):
                        xp_ahead(u + (3 + i) // 2, (3 + i) % 2, (1 + i) % 2, 4 * u + (4 + 2 * i))
                        if ffn:
                            for c in range(4 * i, 4 * i + 4):
                                next_tile(0, u - u0, c)
            half_steps(0, 3, False)
            first_tiles(0)
            half_steps(3, 9, True)
            half_steps(12, 2, False)
            xp_ahead(15, 1, 1, 2 * 30)

            sp.wait_ge(s_res, 1)
            sp.dma_start(res_d, X2).then_inc(s_resst, 16)
            sp.wait_ge(s_route, 2)

            def conv_matrices(cv):
                with sp.Fori(0, D // 16) as u:
                    for s in range(2):
                        sp.wait_ge(s_cmm, 2 * u + (16 * cv + s + 1))
                        src = bass.AP(kpad[cv].tensor, (2 * u + s) * (8 * 3 * TAPS) + cv,
                                      [[1, P], [3 * TAPS, 8], [1, 2 * P]])
                        sp.dma_start(tp[:, s, :, :], src).then_inc(s_tp[s], 16)

            conv_matrices(0)
            sp.wait_ge(s_cmm, 16 + CR)
            first_tiles(1)
            with sp.Fori(0, NF // 8) as u:
                for c in range(8):
                    next_tile(1, u, c)
            for s in range(4):
                sp.wait_ge(s_w[s], 48 * (NFL // 4) * 2)
            conv_matrices(1)
            sp.wait_ge(s_cev, 32 + CR)
            sp.wait_ge(s_resst, 16)
            sp.dma_start(X2, res_d).then_inc(s_resld, 16)
            for i in range(8):
                sp.wait_ge(s_fin, i + 1)
                k, b0 = i // 4, (i % 4) * 8
                sp.dma_start(out_v[:, k, b0:b0 + 8, :], X[:, 8 * i:8 * i + 8, :]).then_inc(s_out, 16)
            sp.wait_ge(s_out, 16 * 8)
            for s in range(4):
                sp.wait_ge(s_st[s], 16 * (2 * NF // 4 + 1))

        @block.gpsimd
        def _(pool):
            pool.sem_inc(s_xncp, CR)

            def copy_xn(layer):
                with pool.Fori(0, NT // 8) as u:
                    for s in range(2):
                        pool.wait_ge(s_xg, 2 * u + (16 * layer + s + 1))
                        pool.tensor_copy(XN[:, ds(8 * u + 4 * s, 4), :].rearrange("p a d -> p (a d)"),
                                         xg[:, s, :]).then_inc(s_xncp, 1)

            def scatter(layer):
                pool.wait_ge(s_route, layer + 1)
                pool.wait_ge(s_xncp, 16 * (layer + 1) + CR)
                if layer == 0:
                    pool.wait_ge(s_zf, 64)
                else:
                    for s in range(4):
                        pool.wait_ge(s_w[s], 48 * NFL // 4)
                for j in range(NT):
                    for k in range(2):
                        pool.indirect_dma_start(
                            sorted_x, bass.IndirectOffsetOnAxis(ap=idx[:, k, j:j + 1], axis=0),
                            XN[:, j, :], None).then_inc(s_sc, 16)

            def gather(layer):
                pool.wait_ge(s_sc, 16 * 2 * NT * (layer + 1))
                for s in range(4):
                    pool.wait_ge(s_st[s], 16 * (NF // 4 * (layer + 1) + 1))
                    pool.wait_ge(s_w[s], 48 * (NFL // 4) * (layer + 1))
                for j in range(NT):
                    if j % 8 == 0 and j >= 16:
                        pool.wait_ge(s_comb, 8 * layer + j // 8 - 1)
                    for k, dst in ((0, XN[:, j, :]), (1, Y2[:, j % 16, :])):
                        pool.indirect_dma_start(
                            dst, None, sorted_y,
                            bass.IndirectOffsetOnAxis(ap=idx[:, k, j:j + 1], axis=0)).then_inc(s_gy[j // 8 % 2], 16)

            copy_xn(0)
            scatter(0)
            for b in range(B1, B2):
                s = b % 2
                pool.wait_ge(s_qkv, 2 * b + 3)
                pool.wait_ge(s_on, b - 1)
                for t in range(2):
                    last = qk_product(pool, s, t)
                last.then_inc(s_pp, 1)
            gather(0)
            copy_xn(1)
            scatter(1)
            gather(1)

        @block.scalar
        def _(act):
            act.dma_start(cst[:, :], consts).then_inc(s_cst, 16)
            act.dma_start(w1s[:, :], w128).then_inc(s_cst, 16)
            act.dma_start(w3s[:, :], w32).then_inc(s_cst, 16)
            act.dma_start(rws[:, :], rows).then_inc(s_cst, 16)
            act.sem_inc(s_xt, CR)
            act.sem_inc(s_yev, CR)
            act.sem_inc(s_qkv, 1)
            for s in range(4):
                act.sem_inc(s_st[s], 16)
            for s in range(2):
                act.sem_inc(s_xtst[s], 16)
            act.sem_inc(s_xsT, CR)
            act.sem_inc(s_gelu, CR)
            act.sem_inc(s_hT, CR)
            act.sem_inc(s_cT, CR)
            act.sem_inc(s_cg, CR)

            def copy_xT(layer):
                with act.Fori(0, NT // 8) as u:
                    for s in range(2):
                        g = 2 * u + (16 * layer + s)
                        act.wait_ge(s_tr, g + (1 + CR))
                        act.wait_ge(s_gate, g + 1)
                        if layer == 0:
                            act.wait_ge(s_xtst[s], 16 * u + 16)
                        act.copy(xT[:, s, :], psH[s][:, :]).then_inc(s_xt, 1)

            def rows_T(layer, v, c):
                s = c % 2
                F = 8 * v + (c + layer * NF)
                act.wait_ge(s_XT, F + 1)
                act.wait_ge(s_H, 2 * F + 2)
                act.copy(xsT[:, s, :], psT[:, 0:FT]).then_inc(s_xsT, 1)

            def gelus(layer, v, c):
                s = c % 2
                F = 8 * v + (c + layer * NF)
                act.wait_ge(s_Y, F + 1)
                for m in range(MK):
                    if m % 2 == 0:
                        act.wait_ge(s_H, 2 * F + (5 + m // 2))
                    g = act.activation(hT[:, s, m, :], psH[2 * s + m // 2][:, (m % 2) * FT:(m % 2 + 1) * FT],
                                       ACT.Gelu, bias=wc[:, c % 4, HID + MK * D + m:HID + MK * D + m + 1])
                g.then_inc(s_gelu, 1)

            def expert_evac(layer, v, c):
                F = 8 * v + (c + layer * NF)
                stored = 32 * v + 16 * (c // 4 + layer * (NF // 4) + 1)
                act.wait_ge(s_Y, F + (1 + CR))
                act.wait_ge(s_st[c % 4], stored)
                act.copy(ys[:, c % 4, :], psY[:, 0:FT]).then_inc(s_yev, 1)

            def evac_qkv(m, s, t):
                act.wait_ge(s_qps, 2 * m + (t + 1))
                if t == 0 and not isinstance(m, int):
                    act.wait_ge(s_on, m - 1)
                act.copy(qkv[:, s, t, :], psQ[:, 0:3 * D]).then_inc(s_qkv, 1)

            def std_dev(n):
                act.wait_ge(s_var, n)
                act.activation(sdev[:, :], var[:, :], ACT.Sqrt).then_inc(s_rstd, 1)

            def pair_heads(b):
                act.wait_ge(s_ot, b + 1)
                act.copy(OT, psA[:, 0:256]).then_inc(s_otsb, 1)

            def pair_exp(b):
                act.wait_ge(s_sub, b + 1)
                act.activation(Pr, S, ACT.Exp, scale=SCALE).then_inc(s_exp, 1)

            def half_steps(u0, n, ffn):
                with act.Fori(u0, u0 + n) as u:
                    if ffn:
                        rows_T(0, u - u0, 0)
                    for i in range(2):
                        b, s = 2 * u + (1 + i), i % 2
                        if ffn:
                            for c in range(4 * i, 4 * i + 4):
                                gelus(0, u - u0, c)
                                if c < 7:
                                    rows_T(0, u - u0, c + 1)
                                if c > 0:
                                    expert_evac(0, u - u0, c - 1)
                                if c % 4 == 0:
                                    pair_heads(b)
                                    evac_qkv(b + 1, s, 0)
                                if c % 4 == 1:
                                    evac_qkv(b + 1, s, 1)
                                    pair_exp(b)
                        else:
                            pair_heads(b)
                            evac_qkv(b + 1, s, 0)
                            evac_qkv(b + 1, s, 1)
                            pair_exp(b)
                    if ffn:
                        expert_evac(0, u - u0, 7)

            std_dev(1)
            copy_xT(0)
            act.wait_ge(s_rin, 1)
            act.activation(stats[:, :, 4], stats[:, :, 4], ACT.Exp).then_inc(s_ex, 1)
            act.wait_ge(s_zf, 64)
            for m in range(2):
                for t in range(2):
                    evac_qkv(m, m, t)
            pair_exp(0)
            half_steps(0, 3, False)
            half_steps(3, 9, True)
            half_steps(12, 3, False)
            pair_heads(NPAIR - 1)
            pair_exp(NPAIR - 1)
            pair_heads(NPAIR)
            std_dev(2)
            copy_xT(1)
            act.wait_ge(s_rin, 2)
            lg = rt[7].rearrange("p j e -> p (j e)")
            act.activation(lg, lg, ACT.Exp).then_inc(s_ex, 1)
            std_dev(3)
            with act.Fori(0, NT // 8) as u:
                for s in range(2):
                    act.wait_ge(s_htr, 2 * u + (s + 1 + CR))
                    act.wait_ge(s_pps, 8 * u + 4 * (s + 1))
                    aff = dict(scale=w1s[:, W_GAM:W_GAM + 1], bias=w1s[:, W_BET:W_BET + 1])
                    act.activation(xT[:, s, :], psH[s][:, :], ACT.Identity, **aff)
                    act.activation(xTr[:, s, :].rearrange("p (k n) -> p k n", k=4),
                                   psH[s][:, :].rearrange("p (k n) -> p k n", k=4)[:, :, ::-1],
                                   ACT.Identity, **aff).then_inc(s_hT, 1)
            with act.Fori(0, NF // 8) as u:
                rows_T(1, u, 0)
                for c in range(8):
                    gelus(1, u, c)
                    if c < 7:
                        rows_T(1, u, c + 1)
                    if c > 0:
                        expert_evac(1, u, c - 1)
                expert_evac(1, u, 7)
            act.wait_ge(s_cev, 32 + CR)
            with act.Fori(0, NT // 8) as u:
                for s in range(2):
                    act.wait_ge(s_ctr, 2 * u + (s + 1))
                    act.copy(xg[:, s, :].rearrange("p (j d) -> p j d", j=4), Vj[:, ds(8 * u + 4 * s, 4), :])\
                        .then_inc(s_cg, 1)
                    act.wait_ge(s_ctr, 2 * u + (s + 1 + CR))
                    act.wait_ge(s_ops, 2 * u + (s + 1))
                    act.copy(xT[:, s, :], psH[s][:, :]).then_inc(s_cT, 1)

        @block.tensor
        def _(pe):
            pe.wait_ge(s_cst, 64)
            pe.wait_ge(s_set, 1)
            pe.matmul(ps[0][:, 0:2 * D], w3s[:, 0:P], w3s[:, P:P + 2 * D], start=True, stop=True).then_inc(s_wps, 1)
            one = ones[0:1, :]
            pe.matmul(ps[1][:, 0:D], one, rws[:, R_BQ:R_BQ + D], start=True, stop=True)
            pe.matmul(ps[1][:, D:3 * D], bdn[:, :], w3s[:, P:P + 2 * D], start=True, stop=False)
            pe.matmul(ps[1][:, D:3 * D], one, rws[:, R_BUP:R_BUP + 2 * D], start=False, stop=True)
            pe.matmul(ps[3][:, 0:D], one, rws[:, R_BO0:R_BO0 + D], start=True, stop=True)
            pe.matmul(ps[3][:, D:2 * D], one, rws[:, R_BO1:R_BO1 + D], start=True, stop=True)
            pe.matmul(ps[2][:, 0:3 * D], one, rws[:, R_BIN1:R_BIN1 + 3 * D], start=True, stop=True).then_inc(s_bps, 1)
            pe.wait_ge(s_set, 2)
            pe.sem_inc(s_tr, CR)
            pe.sem_inc(s_gate, CR)
            pe.sem_inc(s_H, 2 * CR)
            pe.sem_inc(s_Y, CR)
            pe.sem_inc(s_ot, 1)
            pe.sem_inc(s_htr, CR)
            pe.sem_inc(s_pps, 8)
            pe.sem_inc(s_cmm, CR)
            pe.sem_inc(s_ctr, CR)
            pe.sem_inc(s_ops, CR)

            def transposes_and_gates(layer, wg):
                if layer == 1:
                    pe.wait_ge(s_xup, NPAIR + 1)
                    pe.wait_ge(s_qkv, 2 * NPAIR + 1)
                with pe.Fori(0, NT // 8) as u:
                    for s in range(2):
                        g = 2 * u + (16 * layer + s)
                        pe.wait_ge(s_xg, g + 1)
                        pe.wait_ge(s_xt, g + 1)
                        for k in range(4):
                            t = pe.transpose(psH[s][:, k * P:(k + 1) * P], xg[:, s, k * P:(k + 1) * P], ident)
                        t.then_inc(s_tr, 1)
                        pe.wait_ge(s_xt, g + (1 + CR))
                        for k in range(4):
                            t = pe.matmul(psQ[:, ds(64 * u + (32 * s + 8 * k), E)], xT[:, s, k * P:(k + 1) * P],
                                          w1s[:, wg:wg + E], start=True, stop=True)
                        t.then_inc(s_gate, 1)

            def route_counts(layer):
                pe.wait_ge(s_rank, layer + 1)
                pe.matmul(psA[:, 0:E], tri, small[:, 0, :], start=True, stop=True)
                pe.matmul(psA[:, E:2 * E], ones[:, :], small[:, 0, :], start=True, stop=True).then_inc(s_tot, 1)

            def rows_X(layer, v, c):
                F = 8 * v + (c + layer * NF)
                loads = 96 * v + 48 * (c // 4 + 1 + layer * (NFL // 4))
                pe.wait_ge(s_w[c % 4], loads)
                pe.wait_ge(s_xsT, F + CR)
                for r in range(FR):
                    t = pe.transpose(psT[:, r * P:(r + 1) * P],
                                     xs[:, c % 4, r * P:(r + 1) * P], ident)
                t.then_inc(s_XT, 1)

            def hidden(layer, v, c):
                s = c % 2
                F = 8 * v + (c + layer * NF)
                pe.wait_ge(s_xsT, F + (1 + CR))
                pe.wait_ge(s_gelu, F + 1)
                for m in range(MK):
                    t = pe.matmul(psH[2 * s + m // 2][:, (m % 2) * FT:(m % 2 + 1) * FT],
                                  wc[:, c % 4, m * P:(m + 1) * P], xsT[:, s, :], start=True, stop=True)
                    if m % 2 == 1:
                        t.then_inc(s_H, 1)

            def expert_out(layer, v, c):
                s = c % 2
                F = 8 * v + (c + layer * NF)
                pe.wait_ge(s_gelu, F + (1 + CR))
                pe.wait_ge(s_yev, F + CR)
                for r in range(FR):
                    pe.matmul(psY[:, r * P:(r + 1) * P], ones3[:, :], bo[:, c % 4, :], start=True, stop=False)
                    for m in range(MK):
                        t = pe.matmul(psY[:, r * P:(r + 1) * P],
                                      hT[:, s, m, r * P:(r + 1) * P],
                                      wc[:, c % 4, HID + m * D:HID + (m + 1) * D],
                                      start=False, stop=(m == MK - 1))
                t.then_inc(s_Y, 1)

            def heads(b):
                pe.wait_ge(s_on, b)
                pe.wait_ge(s_xup, b)
                for t in range(2):
                    i = pe.transpose(psA[:, t * P:(t + 1) * P], On[:, t * P:(t + 1) * P], ident)
                i.then_inc(s_ot, 1)
                pe.wait_ge(s_otsb, b + 1)
                for t in range(2):
                    o = psA[:, 256 + t * P:256 + (t + 1) * P]
                    pe.matmul(o, ones3[:, :], b3[:, 3 * D:4 * D], start=True, stop=False)
                    i = pe.matmul(o, OT[:, t * P:(t + 1) * P], w1s[:, W_O0:W_O0 + D], start=False, stop=True)
                i.then_inc(s_ao, 1)

            def qkv_tile(m, s, t, loads):
                if t == 0:
                    pe.wait_ge(s_xp[s], loads)
                pe.wait_ge(s_qkv, 2 * m + (t + 1))
                pe.matmul(psQ[:, 0:3 * D], ones3[:, :], b3[:, 0:3 * D], start=True, stop=False)
                pe.matmul(psQ[:, 0:3 * D], xp[:, s, t * P:(t + 1) * P], wqkv[:, :], start=False, stop=True)\
                    .then_inc(s_qps, 1)

            def half_steps(u0, n, ffn):
                with pe.Fori(u0, u0 + n) as u:
                    if ffn:
                        rows_X(0, u - u0, 0)
                    for i in range(2):
                        b = 2 * u + (1 + i)
                        m, s = b + 1, i % 2
                        loads = 16 * u + 16 * 2
                        if ffn:
                            for c in range(4 * i, 4 * i + 4):
                                hidden(0, u - u0, c)
                                if c < 7:
                                    rows_X(0, u - u0, c + 1)
                                if c > 0:
                                    expert_out(0, u - u0, c - 1)
                                if c % 4 == 0:
                                    heads(b)
                                    qkv_tile(m, s, 0, loads)
                                if c % 4 == 1:
                                    qkv_tile(m, s, 1, loads)
                        else:
                            heads(b)
                            qkv_tile(m, s, 0, loads)
                            qkv_tile(m, s, 1, loads)
                    if ffn:
                        expert_out(0, u - u0, 7)

            transposes_and_gates(0, W_G0)
            route_counts(0)
            pe.wait_ge(s_route, 1)
            for t in range(2):
                qkv_tile(0, 0, t, 16)
            for t in range(2):
                qkv_tile(1, 1, t, 16)
            half_steps(0, 3, False)
            half_steps(3, 9, True)
            half_steps(12, 3, False)
            heads(NPAIR - 1)
            heads(NPAIR)
            transposes_and_gates(1, W_G1)
            route_counts(1)
            with pe.Fori(0, NT // 8) as u:
                for s in range(2):
                    pe.wait_ge(s_hg, 2 * u + (s + 1))
                    pe.wait_ge(s_hT, 2 * u + (s + 1))
                    for k in range(4):
                        t = pe.transpose(psH[s][:, k * P:(k + 1) * P], xg[:, s, k * P:(k + 1) * P], ident)
                    t.then_inc(s_htr, 1)
                    pe.wait_ge(s_hT, 2 * u + (s + 1 + CR))
                    for k in range(4):
                        pe.wait_ge(s_pev, 8 * u + (4 * s + k + 1))
                        for q, src in ((0, xT), (1, xTr), (2, xT)):
                            t = pe.matmul(psH[2 + k % 2][:, q * D:(q + 1) * D], src[:, s, k * P:(k + 1) * P],
                                          w1s[:, W_IN1 + q * D:W_IN1 + (q + 1) * D], start=True, stop=True)
                        t.then_inc(s_pps, 1)
            pe.wait_ge(s_pev, NT + CR)
            def convolution(cv):
                diag = P if cv == 0 else 0
                with pe.Fori(0, 8) as u:
                    for s in range(2):
                        pe.wait_ge(s_tp[s], 16 * u + (16 * 8 * cv + 16))
                        pe.wait_ge(s_cev, 2 * u + (16 * cv + s + 1))
                        for k in range(8):
                            v = V[:, ds(1024 * u + (512 * s + 64 * k), NT)]
                            v0 = V[:, ds(1024 * u + (512 * s + 64 * k), NT // 2)]
                            pe.matmul(psC[s][:, k * NT:(k + 1) * NT], tp[:, s, k, diag:diag + P], v, start=True, stop=False)
                            t = pe.matmul(psC[s][:, k * NT + NT // 2:(k + 1) * NT], tp[:, s, k, P - diag:2 * P - diag], v0,
                                          start=False, stop=True)
                        t.then_inc(s_cmm, 1)

            convolution(0)
            with pe.Fori(0, NF // 8) as u:
                rows_X(1, u, 0)
                for c in range(8):
                    hidden(1, u, c)
                    if c < 7:
                        rows_X(1, u, c + 1)
                    if c > 0:
                        expert_out(1, u, c - 1)
                expert_out(1, u, 7)
            convolution(1)
            with pe.Fori(0, NT // 8) as u:
                for s in range(2):
                    pe.wait_ge(s_cg, 2 * u + (s + 1 + CR))
                    pe.wait_ge(s_cT, 2 * u + (s + 1))
                    for k in range(4):
                        t = pe.transpose(psH[s][:, k * P:(k + 1) * P], xg[:, s, k * P:(k + 1) * P], ident)
                    t.then_inc(s_ctr, 1)
                    pe.wait_ge(s_cT, 2 * u + (s + 1 + CR))
                    pe.wait_ge(s_oev, 2 * u + (s + 1))
                    for k in range(4):
                        o = psH[2 + s][:, k * P:(k + 1) * P]
                        pe.matmul(o, ones3[:, :], b3[:, 4 * D:5 * D], start=True, stop=False)
                        t = pe.matmul(o, xT[:, s, k * P:(k + 1) * P], w1s[:, W_O1:W_O1 + D], start=False, stop=True)
                    t.then_inc(s_ops, 1)

        @block.vector
        def _(dve):
            steps = [0]

            def link(ins):
                steps[0] += 1
                ins.then_inc(s_v, 1)
                dve.wait_ge(s_v, steps[0])

            zrow = NFL * D * FR // 4
            dve.memset(BG[:, 0:zrow], 0.0).then_inc(s_zero, 1)
            dve.memset(ones[:, :], 1.0)
            link(dve.memset(ones3[:, :], 1.0))
            dve.sem_inc(s_pev, CR)
            dve.sem_inc(s_cev, CR)
            dve.sem_inc(s_oev, CR)
            dve.sem_inc(s_xup, 1)
            dve.sem_inc(s_otsb, 1)

            def in_three_parts(dst, src, n):
                link(dve.tensor_copy(partb[:, 0:n], src))
                link(dve.scalar_tensor_tensor(out=part[:, 0:n], in0=partb[:, 0:n], scalar=cst[0:3, C_M1:C_M1 + 1],
                                              in1=src, op0=ALU.mult, op1=ALU.add))
                link(dve.tensor_copy(partb[:, 0:n], part[:, 0:n]))
                link(dve.scalar_tensor_tensor(out=part[:, 0:n], in0=partb[:, 0:n], scalar=cst[0:3, C_M2:C_M2 + 1],
                                              in1=part[:, 0:n], op0=ALU.mult, op1=ALU.add))
                link(dve.tensor_copy(dst, part[:, 0:n]))

            def fused_weights():
                dve.wait_ge(s_cst, 64)
                dve.tensor_copy(bdn[:, :], w3s[:, P + 2 * D:P + 2 * D + 1].to_broadcast([LAT, P])).then_inc(s_set, 1)
                dve.wait_ge(s_wps, 1)
                dve.tensor_copy(wqkv[:, 0:D], w1s[:, W_Q:W_Q + D])
                dve.tensor_copy(wqkv[:, D:3 * D], ps[0][:, 0:2 * D])
                dve.wait_ge(s_bps, 1)
                dve.tensor_copy(brow[:, 0:3 * D], ps[1][0:3, 0:3 * D])
                dve.tensor_copy(brow[:, 3 * D:5 * D], ps[3][0:3, 0:2 * D])
                link(dve.tensor_copy(bprj[:, :], ps[2][:, 0:3 * D]))
                in_three_parts(b3[:, :], brow[:, :], 5 * D)
                dve.sem_inc(s_set, 1)

            def norm_stats(src, n):
                for j in range(NT):
                    if n == 1 and j % 16 == 0:
                        dve.wait_ge(s_x[j // 16], 16)
                    dve.bn_stats(stats[:, j, :], src[:, j, :])
                link(dve.memset(tmp[:, 0:1], 0.0))
                me, qe, mo, qo = (stats[:, :, i] for i in (1, 2, 4, 5))
                dve.tensor_tensor(mean[:, :], me, mo, ALU.add)
                link(dve.tensor_tensor(tmp[:, :], me, mo, ALU.subtract))
                dve.tensor_tensor(var[:, :], qe, qo, ALU.add)
                link(dve.tensor_tensor(tmp[:, :], tmp[:, :], tmp[:, :], ALU.mult))
                dve.tensor_scalar(mean[:, :], mean[:, :], 0.5, None, ALU.mult)
                link(dve.tensor_scalar(tmp[:, :], tmp[:, :], 0.25, EPS, ALU.mult, ALU.add))
                dve.scalar_tensor_tensor(out=var[:, :], in0=var[:, :], scalar=1.0 / D, in1=tmp[:, :],
                                         op0=ALU.mult, op1=ALU.add).then_inc(s_var, 1)
                dve.wait_ge(s_rstd, n)
                link(dve.reciprocal(rstd[:, :], sdev[:, :]))
                link(dve.tensor_tensor(tmp[:, :], rstd[:, :], rstd[:, :], ALU.mult))
                link(dve.tensor_tensor(tmp[:, :], tmp[:, :], var[:, :], ALU.mult))
                link(dve.tensor_scalar(tmp[:, :], tmp[:, :], -0.5, 1.5, ALU.mult, ALU.add))
                link(dve.tensor_tensor(rstd[:, :], rstd[:, :], tmp[:, :], ALU.mult))

            def normalise(src, g, done):
                for k in range(4):
                    j = 4 * g + k
                    t = dve.tensor_scalar(xg[:, g % 2, k * D:(k + 1) * D], src[:, j, :],
                                          mean[:, j:j + 1], rstd[:, j:j + 1], ALU.subtract, ALU.mult)
                t.then_inc(done, 1)

            def norm_and_transpose(layer):
                for g in range(NT // 4):
                    dve.wait_ge(s_tr, 16 * layer + g + 1)
                    dve.wait_ge(s_xncp, 16 * layer + g + 1)
                    normalise(X, g, s_xg)

            def bt(ap, n):
                return ap[:, :, None].to_broadcast([P, NT, n])

            def be(ap):
                return ap[:, None, :].to_broadcast([P, NT, E])

            def route(layer):
                dve.wait_ge(s_gate, 16 * (layer + 1) + CR)
                L, oh1, oh2, t0, t1, Mk, C, L0 = rt[0:8]
                lg = psQ[:, :].rearrange("p (j e) -> p j e", e=E)
                m1, m2, k1, k2, ta, tb = (stats[:, :, i] for i in range(6))
                if layer == 0:
                    link(dve.tensor_copy(L, lg))
                else:
                    link(dve.tensor_copy(L0, lg))
                    link(dve.tensor_reduce(m1, L0, AX.X, ALU.max))
                    link(dve.tensor_tensor(L0, L0, bt(m1, E), ALU.subtract))
                    dve.sem_inc(s_rin, 1)
                    dve.wait_ge(s_ex, 2)
                    link(dve.tensor_reduce(m1, L0, AX.X, ALU.add))
                    link(dve.reciprocal(m2, m1))
                    link(dve.tensor_tensor(L, L0, bt(m2, E), ALU.mult))
                for m, k, oh in ((m1, k1, oh1), (m2, k2, oh2)):
                    link(dve.tensor_reduce(m, L, AX.X, ALU.max))
                    link(dve.tensor_tensor(t0, L, bt(m, E), ALU.is_equal))
                    link(dve.tensor_tensor(t0, t0, be(rank8), ALU.mult))
                    link(dve.tensor_reduce(k, t0, AX.X, ALU.max))
                    link(dve.tensor_tensor(oh, be(rank8), bt(k, E), ALU.is_equal))
                    if m is m1:
                        link(dve.tensor_scalar(t1, oh, BIG, None, ALU.mult))
                        link(dve.tensor_tensor(L, L, t1, ALU.subtract))
                if layer == 0:
                    link(dve.tensor_tensor(ta, m2, m1, ALU.subtract))
                    dve.sem_inc(s_rin, 1)
                    dve.wait_ge(s_ex, 1)
                    link(dve.tensor_scalar(tb, ta, 1.0, None, ALU.add))
                    link(dve.reciprocal(wt[:, 0, :], tb))
                    link(dve.tensor_tensor(wt[:, 1, :], ta, wt[:, 0, :], ALU.mult))
                else:
                    link(dve.tensor_tensor(ta, m1, m2, ALU.add))
                    link(dve.tensor_scalar(ta, ta, 1e-9, None, ALU.add))
                    link(dve.reciprocal(tb, ta))
                    dve.tensor_tensor(wt[:, 0, :], m1, tb, ALU.mult)
                    link(dve.tensor_tensor(wt[:, 1, :], m2, tb, ALU.mult))
                link(dve.tensor_tensor(Mk, oh1, oh2, ALU.add))
                for e in range(E):
                    sc = dve.tensor_tensor_scan(C[:, :, e], ones[:, 0:NT], Mk[:, :, e], 0.0, ALU.mult, ALU.add)
                link(sc)
                dve.tensor_copy(small[:, 0, :], C[:, NT - 1, :]).then_inc(s_rank, 1)
                dve.wait_ge(s_tot, layer + 1)
                link(dve.tensor_copy(small[:, 1:3, :].rearrange("p a e -> p (a e)"), psA[:, 0:2 * E]))
                base, tot, nt, end, off = (small[:, i, :] for i in range(1, 6))
                cmp = rcmp[:, 0:E * NTHR].rearrange("p (e q) -> p e q", e=E)
                link(dve.tensor_tensor(cmp, tot[:, :, None].to_broadcast([P, E, NTHR]),
                                       thr[:, None, :].to_broadcast([P, E, NTHR]), ALU.is_gt))
                link(dve.tensor_reduce(nt, cmp, AX.X, ALU.add))
                link(dve.tensor_tensor_scan(end, ones[:, 0:E], nt, 0.0, ALU.mult, ALU.add))
                link(dve.tensor_tensor(off, end, nt, ALU.subtract))
                link(dve.tensor_scalar(off, off, float(FT), -1.0, ALU.mult, ALU.add))
                link(dve.tensor_tensor(off, off, base, ALU.add))
                link(dve.tensor_tensor(C, C, be(off), ALU.add))
                for k, oh in ((0, oh1), (1, oh2)):
                    link(dve.tensor_tensor(t0, C, oh, ALU.mult))
                    link(dve.tensor_reduce(ta, t0, AX.X, ALU.add))
                    link(dve.tensor_copy(idx[:, k, :], ta))
                ecmp = rcmp[:, 0:NFL * E].rearrange("p (f e) -> p f e", e=E)
                link(dve.tensor_tensor(ecmp, iota[:, :, None].to_broadcast([P, NFL, E]),
                                       end[:, None, :].to_broadcast([P, NFL, E]), ALU.is_ge))
                link(dve.tensor_reduce(L.rearrange("p j e -> p (j e)")[:, 0:NFL], ecmp, AX.X, ALU.add))
                dve.tensor_scalar(eid[:, :], L.rearrange("p j e -> p (j e)")[:, 0:NFL], float(E - 1), None,
                                  ALU.min).then_inc(s_route, 1)

            def add_heads(b):
                dve.wait_ge(s_ao, b)
                xv = X[:, ds(2 * b - 2, 2), :].rearrange("p a d -> p (a d)")
                dve.tensor_tensor(xv, xv, psA[:, 256:512], ALU.add).then_inc(s_xup, 1)

            def combine(layer, i, par, gathered):
                dve.wait_ge(s_gy[par], gathered)
                for k in range(2):
                    for c in range(8):
                        j = 8 * i + c
                        y1 = XN[:, ds(j, 1), :].rearrange("p a d -> p (a d)")
                        acc = y1 if layer else X[:, ds(j, 1), :].rearrange("p a d -> p (a d)")
                        w = wt[:, k, ds(j, 1)]
                        if layer and k == 0:
                            t = dve.tensor_scalar(acc, y1, w, None, ALU.mult)
                        else:
                            t = dve.scalar_tensor_tensor(out=acc, in0=Y2[:, 8 * par + c, :] if k else y1, scalar=w,
                                                         in1=acc, op0=ALU.mult, op1=ALU.add)
                    t.then_inc(s_comb1 if k == 0 else s_comb, 1)
                    dve.wait_ge(s_comb1 if k == 0 else s_comb, i + (8 * layer + 1))

            def pair(b, s, skipped=0, on_pool=False, first=False, combines=None):
                def step(n, ins):
                    ins.then_inc(s_att, 1)
                    dve.wait_ge(s_att, K_ATT * b + n)

                if on_pool:
                    dve.wait_ge(s_pp, b - (B1 - 1))
                else:
                    dve.wait_ge(s_qkv, 2 * b + 3)
                    for t in range(2):
                        i = qk_product(dve, s, t)
                    i.then_inc(s_vp, 1)
                    dve.wait_ge(s_vp, b + (1 - skipped))
                step(1, dve.tensor_reduce(S, prod[:, s, :].rearrange("p (n d) -> p n d", d=DH), AX.X, ALU.add))
                S3 = S.rearrange("p (n g) -> p n g", g=H)
                step(2, dve.tensor_reduce(Mx, S3, AX.X, ALU.max))
                dve.tensor_tensor(S3, S3, Mx[:, :, None].to_broadcast([P, 2 * H, H]), ALU.subtract).then_inc(s_sub, 1)
                if not first:
                    add_heads(b)
                dve.wait_ge(s_exp, b + 1)
                P3 = Pr.rearrange("p (n g) -> p n g", g=H)
                step(3, dve.tensor_reduce(Sm, P3, AX.X, ALU.add))
                dve.reciprocal(Rc, Sm)
                for t in range(2):
                    kv = qkv[:, s, t, D:3 * D].rearrange("p (g e) -> p g e", g=H)
                    v = kv[:, :, DH:2 * DH].rearrange("p g e -> p e g")
                    i = dve.tensor_tensor(
                        prod[:, s, t * 2048:(t + 1) * 2048].rearrange("p (h e g) -> p h e g", h=H, e=DH),
                        Pr[:, t * 256:(t + 1) * 256].rearrange("p (h g) -> p h g", h=H)[:, :, None, :]
                        .to_broadcast([P, H, DH, H]),
                        v[:, None, :, :].to_broadcast([P, H, DH, H]), ALU.mult)
                step(4, i)
                step(5, dve.tensor_reduce(O, prod[:, s, :].rearrange("p (n g) -> p n g", g=H), AX.X, ALU.add))
                dve.wait_ge(s_ot, b + 1)
                dve.tensor_tensor(On.rearrange("p (n e) -> p n e", e=DH), O.rearrange("p (n e) -> p n e", e=DH),
                                  Rc[:, :, None].to_broadcast([P, 2 * H, DH]), ALU.mult).then_inc(s_on, 1)
                if combines is not None:
                    combine(0, *combines)

            def half_steps(u0, n, ffn, comb=False):
                with dve.Fori(u0, u0 + n) as u:
                    for i in range(2):
                        pair(2 * u + (1 + i), (1 + i) % 2, B2 - B1 if comb else 0, on_pool=ffn,
                             combines=(2 * u + (i - 2 * u0), i, 256 * u + 256 * (1 - u0)) if comb else None)

            norm_stats(X, 1)
            fused_weights()
            norm_and_transpose(0)
            dve.wait_ge(s_bf, 32)
            for layer in range(2):
                in_three_parts(bout3[:, layer, :], boutf[:, layer, :], E * D)
            dve.sem_inc(s_bo3, 1)
            dve.wait_ge(s_bo3st, 32)
            route(0)
            pair(0, 0, first=True)
            half_steps(0, 3, False)
            half_steps(3, 9, True)
            half_steps(12, 3, False, comb=True)
            pair(NPAIR - 1, 1, B2 - B1, combines=(6, 0, 256 * 4))
            add_heads(NPAIR)
            dve.wait_ge(s_xup, NPAIR + 1)
            combine(0, 7, 1, 256 * 4)

            norm_stats(X, 2)
            norm_and_transpose(1)
            route(1)
            dve.wait_ge(s_xncp, 32 + CR)
            dve.tensor_tensor(X2, X2, XN[:, :, :].rearrange("p j d -> p (j d)"), ALU.add).then_inc(s_res, 1)
            norm_stats(XN, 3)
            normalise(XN, 0, s_hg)
            for g in range(NT // 4):
                if g + 1 < NT // 4:
                    dve.wait_ge(s_htr, g + 2)
                    normalise(XN, g + 1, s_hg)
                if g == 0:
                    dve.wait_ge(s_resst, 16)
                for k in range(4):
                    j = 4 * g + k
                    bank = psH[2 + k % 2]
                    dve.wait_ge(s_pps, j + 1 + 8)
                    dve.tensor_tensor(VX1j[:, j, :], bank[:, 0:2 * D], bprj[:, 0:2 * D], ALU.add)
                    dve.tensor_tensor(X2j[:, j, :], bank[:, 2 * D:3 * D], bprj[:, 2 * D:3 * D], ALU.add)\
                       .then_inc(s_pev, 1)

            def conv_gate(cv, n, s, gate):
                dve.wait_ge(s_cmm, n + (16 * cv + s + 1 + CR))
                sl = ds(512 * n + 512 * s, 512)
                dve.tensor_tensor(V[:, sl], psC[s % 2][:, :], gate[:, sl], ALU.mult).then_inc(s_cev, 1)

            with dve.Fori(0, 8) as u:
                for s in range(2):
                    conv_gate(0, 2 * u, s, X1)
            with dve.Fori(0, 4) as u:
                for s in range(4):
                    conv_gate(1, 4 * u, s, X2)
                    if s % 2 == 1:
                        combine(1, 2 * u + s // 2, s // 2, 256 * u + 256 * 5)
            dve.wait_ge(s_resld, 16)
            with dve.Fori(0, NT // 8) as u:
                for s in range(2):
                    dve.wait_ge(s_ops, 2 * u + (s + 1 + CR))
                    xv = X[:, ds(8 * u + 4 * s, 4), :].rearrange("p a d -> p (a d)")
                    dve.tensor_tensor(xv, xv, psH[2 + s][:, :], ALU.add).then_inc(s_oev, 1)
                dve.wait_ge(s_oev, 2 * u + (2 + CR))
                xv = X[:, ds(8 * u, 8), :].rearrange("p a d -> p (a d)")
                dve.tensor_tensor(xv, xv, XN[:, ds(8 * u, 8), :].rearrange("p a d -> p (a d)"), ALU.add)\
                   .then_inc(s_fin, 1)


def kernel(**inputs):
    import numpy as _np
    import concourse.bacc as _bacc
    from concourse import mybir as _mybir
    from concourse.bass_utils import run_bass_kernel_spmd as _run

    a = {k: _np.asarray(v) for k, v in inputs.items()}
    consts = _np.concatenate([
        _np.eye(P), _np.triu(_np.ones((P, P)), 1), _np.tile(_np.arange(E, 0, -1), (P, 1)),
        _np.tile(FT * _np.arange(NTHR), (P, 1)), _np.tile(_np.arange(NFL), (P, 1)),
        -1.0 * (_np.arange(P)[:, None] >= [[1, 2]])], 1).astype(_np.float32)

    def experts(w_in, b_in, w_out):
        return _np.concatenate([w_in, w_out.reshape(E, MK, P, D).transpose(0, 2, 1, 3).reshape(E, P, MK * D),
                                b_in.reshape(E, MK, P).transpose(0, 2, 1)], 2)

    def padded(k):
        return _np.pad(k, ((0, 0), (TAPS, TAPS)))

    arrays = {
        "x": a["L0_attn_x"],
        "consts": consts,
        "w128": _np.concatenate([a["L0_attn_Wq"], a["L0_ffn_W_gate"], a["L0_attn_Wout"], a["L1_attn_W_in"],
                                 a["L1_ffn_gate_w"].T, a["L1_attn_W_out"], a["L1_attn_gamma"][:, None],
                                 a["L1_attn_beta"][:, None]], 1),
        "w32": _np.concatenate([a["L0_attn_Wdown"].T, a["L0_attn_Wup"], a["L0_attn_bdown"][:, None]], 1),
        "rows": _np.concatenate([a["L0_attn_bq"], a["L0_attn_bup"], a["L0_attn_bout"], a["L1_attn_b_in"],
                                 a["L1_attn_b_out"]])[None, :],
        "moe0": experts(a["L0_ffn_W_in"], a["L0_ffn_b_in"], a["L0_ffn_W_out"]),
        "bout0": a["L0_ffn_b_out"],
        "moe1": experts(a["L1_ffn_w1"], a["L1_ffn_b1"], a["L1_ffn_w2"]),
        "bout1": a["L1_ffn_b2"],
        "kpad0": padded(a["L1_attn_k0"][0, :, ::-1]),
        "kpad1": padded(a["L1_attn_k1"][0]),
    }
    nc = _bacc.Bacc("TRN2", target_bir_lowering=False, num_devices=1)
    arrays = {f"in_{k}": _np.ascontiguousarray(v) for k, v in arrays.items()}
    args = [nc.dram_tensor(k, v.shape, _mybir.dt.from_np(v.dtype), kind="ExternalInput").ap()
            for k, v in arrays.items()]
    out = nc.dram_tensor("out_0", (BATCH, TIME, D), _mybir.dt.float32, kind="ExternalOutput").ap()
    mixed_layers(nc, *args, out)
    return _run(nc, [arrays], core_ids=[0]).results[0]["out_0"]
```

```python
import concourse.bass as bass
from concourse import mybir
from contextlib import ExitStack

P = 128
BATCH, TIME, D = 32, 256, 128
BLKS = TIME // P
NT = BATCH * BLKS
H, DH = 16, 8
LAT = 32
E, HID = 8, 512
MK = HID // P
FT = 256
FR = FT // P
NF = 2 * NT * P // FT + E
AHEAD = 4
NFL = NF + AHEAD
ZC = 1024
NZ = NFL * FR * D // ZC
TAPS = 128
SCALE = float(DH) ** -0.5
EPS = 1e-5
BIG = 3.0e38

C_ID, C_TRI, C_R8, C_THR, C_IOTA = 0, P, 2 * P, 2 * P + E, 2 * P + E + NT * P // FT
C_M1 = C_IOTA + NFL
C_M2 = C_M1 + 1
C_END = C_M2 + 1
NTHR = NT * P // FT
W_Q, W_G0, W_O0, W_IN1, W_G1, W_O1, W_GAM, W_BET, W_END = 0, 128, 136, 264, 648, 656, 784, 785, 786
R_BQ, R_BUP, R_BO0, R_BIN1, R_BO1, R_END = 0, 128, 384, 512, 896, 1024
B_QKV, B_O0, B_O1, B_IN1, B_END = 0, 3 * D, 4 * D, 5 * D, 8 * D
WCAT = HID + MK * D + MK


def mixed_layers(nc, x, consts, w128, w32, rows, moe0, bout0, moe1, bout1, kpad0, kpad1, out):
    fp32, bf16, i32, u32 = mybir.dt.float32, mybir.dt.bfloat16, mybir.dt.int32, mybir.dt.uint32
    ALU, ACT, AX = mybir.AluOpType, mybir.ActivationFunctionType, mybir.AxisListType
    ds = bass.ds

    ctx = ExitStack()
    with ctx:
        def sb(name, shape, dt=fp32):
            return ctx.enter_context(nc.sbuf_tensor(name, shape, dt))

        def sem(name):
            return ctx.enter_context(nc.semaphore(name))

        def dram(name, shape, dt=fp32):
            return nc.dram_tensor(name, shape, dt, kind="Internal").ap()

        sorted_x = dram("sorted_x", (NFL * FT, D))
        sorted_y = dram("sorted_y", (NF * FT, D))
        xt_d = dram("xt_d", (NT // 4, P, 4 * P))
        bo3_d = [dram(f"bo3_{n}", (3, E * D), bf16) for n in range(2)]
        res_d = dram("res_d", (P, NT * D))

        X = sb("X", [P, NT, D])
        XN = sb("XN", [P, NT, D])
        BG = sb("BG", [P, 16384])
        FF = sb("FF", [P, 9232])
        cst = sb("cst", [P, C_END])
        w1s = sb("w1s", [P, W_END])
        w3s = sb("w3s", [LAT, LAT + 2 * D + P - LAT + 1])
        rws = sb("rws", [1, R_END])
        ones = sb("ones", [P, P])
        bdn = sb("bdn", [LAT, P])
        wqkv = sb("wqkv", [P, 3 * D])
        brow = sb("brow", [3, B_END])
        b3 = sb("b3", [3, B_END], bf16)
        ones3 = sb("ones3", [3, P], bf16)
        xg = sb("xg", [P, 2, 4 * P])
        xT = sb("xT", [P, 2, 4 * P])
        stats = sb("stats", [P, NT, 6])
        mean = sb("mean", [P, NT])
        rstd = sb("rstd", [P, NT])
        var = sb("var", [P, NT])
        sdev = sb("sdev", [P, NT])
        tmp = sb("tmp", [P, NT])
        wt = sb("wt", [P, 2, NT])
        small = sb("small", [P, 6, E])
        best = sb("best", [P, 6, NT])
        idx = sb("idx", [P, 2, NT], u32)
        eid = sb("eid", [P, NFL], i32)

        ident = cst[:, C_ID:C_ID + P]
        tri = cst[:, C_TRI:C_TRI + P]
        rank8 = cst[:, C_R8:C_R8 + E]
        thr = cst[:, C_THR:C_THR + NTHR]
        iota = cst[:, C_IOTA:C_IOTA + NFL]

        prod = BG[:, 0:8192].rearrange("p (s n) -> p s n", s=2)
        prodv = BG[:, 8192:12288]
        qkv = BG[:, 12288:13824].rearrange("p (s t n) -> p s t n", s=2, t=2)
        xp = BG[:, 13824:14336].rearrange("p (s n) -> p s n", s=2)
        S = BG[:, 14336:15360].rearrange("p (s n) -> p s n", s=2)
        vals = BG[:, 15360:15872].rearrange("p (s t n) -> p s t n", s=2, t=2)
        Mx = BG[:, 15872:15904]
        Sm = BG[:, 15904:15936]
        Rc = BG[:, 15936:15968]
        xg_all = xg[:, :, :].rearrange("p s n -> p (s n)")
        O = xg_all[:, 0:256]
        On = xg_all[:, 256:768].rearrange("p (s n) -> p s n", s=2)
        OT = xg_all[:, 768:1024]

        V = BG[:, 0:8192]
        X1 = BG[:, 8192:16384]
        R = X1.rearrange("p (j d) -> p j d", d=D)
        X2 = X[:, :, :].rearrange("p j d -> p (j d)")
        Vj = V.rearrange("p (d j) -> p j d", j=NT)
        VX1j = BG[:, :].rearrange("p (d j) -> p j d", j=NT)
        X2j = X2.rearrange("p (d j) -> p j d", j=NT)

        wc = FF[:, 0:4 * WCAT].rearrange("p (s n) -> p s n", s=4)
        bo = FF[0:3, 4112:4368].bitcast(bf16).rearrange("p (s n) -> p s n", s=4)
        xs = FF[:, 4624:5648].rearrange("p (s n) -> p s n", s=4)
        xsT = FF[:, 5648:6160].rearrange("p (s n) -> p s n", s=2)
        hT = FF[:, 6160:8208].rearrange("p (s m n) -> p s m n", s=2, m=MK)
        ys = FF[:, 8208:9232].rearrange("p (s n) -> p s n", s=4)
        Y2 = FF[:, 0:2048].rearrange("p (j d) -> p j d", d=D)
        tp = FF[:, 2048:6144].rearrange("p (s c n) -> p s c n", s=2, c=8)
        xTr = FF[:, 6160:7184].rearrange("p (s n) -> p s n", s=2)
        boutf = FF[0:3, 0:2048].rearrange("p (l n) -> p l n", l=2)
        part = FF[0:3, 2048:3072]
        partb = FF[0:3, 3072:3584].bitcast(bf16)
        bout3 = FF[0:3, 3584:4608].bitcast(bf16).rearrange("p (l n) -> p l n", l=2)
        rt = [FF[:, i * 512:(i + 1) * 512].rearrange("p (j e) -> p j e", e=E) for i in range(8)]
        rcmp = FF[:, 5120:5120 + NFL * E]

        ps = [ctx.enter_context(nc.psum_tensor(f"ps{i}", [P, 512], fp32)) for i in range(8)]
        psH = ps[0:4]
        psT, psY, psQ, psA = ps[4:8]
        psC = [psQ, psA]

        CR = 2
        s_x = [sem(f"x_loaded{i}") for i in range(4)]
        s_cst = sem("weights_loaded")
        s_w3 = sem("kv_weights_loaded")
        s_set = sem("setup_done")
        s_wps = sem("fused_weights_psum")
        s_bps = sem("bias_psum")
        s_zero = sem("zeros_ready")
        s_zf = sem("sorted_x_zeroed")
        s_v = sem("vector_step")
        s_bf = sem("bout_loaded")
        s_bo3 = sem("bout_split")
        s_bo3st = sem("bout_parts_stored")
        s_var = sem("variance_ready")
        s_rstd = sem("rstd_ready")
        s_xn = sem("xn_ready")
        s_tr = sem("xn_transposed")
        s_xt = sem("xT_ready")
        s_gate = sem("gate_logits")
        s_xtst = [sem(f"xT_stored{i}") for i in range(2)]
        s_ex = sem("gate_exp")
        s_rin = sem("route_exp_in")
        s_tot = sem("route_totals")
        s_rank = sem("route_counts_in")
        s_rows = sem("row_indices_ready")
        s_route = sem("routed")
        s_sc = sem("rows_scattered")
        s_w = [sem(f"expert_tile_loaded{i}") for i in range(4)]
        s_xs = [sem(f"rows_loaded{i}") for i in range(4)]
        s_st = [sem(f"expert_out_stored{i}") for i in range(4)]
        s_XT = sem("rows_transposed")
        s_xsT = sem("xsT_ready")
        s_H = sem("hidden_psum")
        s_gelu = sem("hidden_ready")
        s_Y = sem("expert_out_psum")
        s_yev = sem("expert_out_ready")
        s_gy = [sem(f"outputs_gathered{i}") for i in range(2)]
        s_xp = [sem(f"xp_loaded{i}") for i in range(2)]
        s_qps = sem("qkv_psum")
        s_qkv = sem("qkv_ready")
        s_pp = sem("pool_products")
        s_vals = sem("values_copied")
        s_att = sem("attention_step")
        s_sub = sem("scores_ready")
        s_exp = sem("probs_ready")
        s_on = sem("heads_ready")
        s_ot = sem("heads_transposed")
        s_otsb = sem("headsT_ready")
        s_ao = sem("attention_out_psum")
        s_xup = sem("attention_added")
        s_scaled = sem("expert_outputs_scaled")
        s_comb1 = sem("first_expert_added")
        s_comb = sem("combined")
        s_vp = sem("vector_products")
        s_res = sem("residual_ready")
        s_resst = sem("residual_stored")
        s_resld = sem("residual_loaded")
        s_hg = sem("hn_ready")
        s_htr = sem("hn_transposed")
        s_hT = sem("hT_ready")
        s_pps = sem("projection_psum")
        s_pev = sem("projection_ready")
        s_tp = [sem(f"toeplitz_loaded{i}") for i in range(2)]
        s_cmm = sem("conv_psum")
        s_cev = sem("conv_ready")
        s_cg = sem("conv_gathered")
        s_ctr = sem("conv_transposed")
        s_cT = sem("convT_ready")
        s_ops = sem("conv_out_psum")
        s_oev = sem("conv_out_added")
        s_out = sem("out_stored")
        block = ctx.enter_context(nc.Block())

        B1, B2 = 7, 25
        NPAIR = NT // 2
        K_ATT = 5

        x_v = x.rearrange("b (k p) d -> p k b d", p=P)
        out_v = out.rearrange("b (k p) d -> p k b d", p=P)
        sx_v = sorted_x.rearrange("(f p r) d -> f p (r d)", p=P, r=FR)
        sy_v = sorted_y.rearrange("(f p r) d -> f p (r d)", p=P, r=FR)
        moe, bout_d, kpad = [moe0, moe1], [bout0, bout1], [kpad0, kpad1]

        def qk_product(eng, s, t):
            q = qkv[:, s, t, 0:D].rearrange("p (h e) -> p h e", h=H)
            k = qkv[:, s, t, D:3 * D].rearrange("p (g e) -> p g e", g=H)[:, :, 0:DH]
            return eng.tensor_tensor(
                prod[:, s, t * 2048:(t + 1) * 2048].rearrange("p (h g e) -> p h g e", h=H, g=H),
                q[:, :, None, :].to_broadcast([P, H, H, DH]), k[:, None, :, :].to_broadcast([P, H, H, DH]), ALU.mult)

        @block.sync
        def _(sp):
            for c in range(4):
                k, b0 = c // 2, (c % 2) * 16
                sp.dma_start(X[:, c * 16:(c + 1) * 16, :], x_v[:, k, b0:b0 + 16, :]).then_inc(s_x[c], 16)
            sp.wait_ge(s_cst, 48)
            sp.wait_ge(s_zero, 1)
            zv = sorted_x.rearrange("(p r) d -> p (r d)", p=P)
            early = NZ - NT // 4
            for c in range(early):
                sp.dma_start(zv[:, c * ZC:(c + 1) * ZC], prodv[:, 0:ZC]).then_inc(s_zf, 16)
            xt_pairs = xt_d.rearrange("g p (h n) -> g h p n", h=2)

            def load_xp(g, h, s):
                sp.dma_start(xp[:, s, :], xt_pairs[ds(g, 1), h, :, :].rearrange("a p n -> p (a n)"))\
                    .then_inc(s_xp[s], 16)

            def store_xt(u):
                for s in range(2):
                    sp.wait_ge(s_xt, 2 * u + (s + 1 + CR))
                    sp.dma_start(xt_d[ds(2 * u + s, 1), :, :].rearrange("a p n -> p (a n)"), xT[:, s, :])\
                        .then_inc(s_xtst[s], 16)
                    sp.dma_start(zv[:, ds(2 * ZC * u + (early + s) * ZC, ZC)], prodv[:, 0:ZC]).then_inc(s_zf, 16)

            store_xt(0)
            sp.wait_ge(s_xtst[0], 32)
            for h in range(2):
                load_xp(0, h, h)
            with sp.Fori(1, NT // 8) as u:
                store_xt(u)
            for s in range(2):
                sp.wait_ge(s_xtst[s], 16 * (NT // 8 + 1))
            sp.wait_ge(s_bo3st, 32)

            def load_rows(f, s):
                sp.dma_start(xs[:, s, :], sx_v[ds(f, 1), :, :].rearrange("a p n -> p (a n)")).then_inc(s_xs[s], 16)

            def expert_of(f):
                return sp.value_load(eid[0:1, ds(f, 1)], min_val=0, max_val=E - 1)

            def load_weights(layer, e, s):
                sp.dma_start(wc[:, s, :], moe[layer][ds(e, 1), :, :].rearrange("a p n -> p (a n)"))\
                    .then_inc(s_w[s], 16)
                sp.dma_start(bo[:, s, :], bo3_d[layer][:, ds(e * D, D)]).then_inc(s_w[s], 16)

            def first_tiles(layer):
                sp.wait_ge(s_route, layer + 1)
                for f in range(AHEAD):
                    load_weights(layer, expert_of(f), f)
                sp.wait_ge(s_sc, 16 * 2 * NT * (layer + 1))
                for f in range(AHEAD):
                    load_rows(f, f)

            def next_tile(layer, v, c):
                f, s = 8 * v + c, c % 4
                sp.wait_ge(s_XT, f + (layer * (NF + 2) + 1))
                load_rows(f + AHEAD, s)
                e = expert_of(f + AHEAD)
                sp.wait_ge(s_yev, f + (layer * NF + 1 + CR))
                load_weights(layer, e, s)
                sp.dma_start(sy_v[ds(f, 1), :, :].rearrange("a p n -> p (a n)"), ys[:, s, :])\
                    .then_inc(s_st[s], 16)

            def xp_ahead(g, h, s, done):
                sp.wait_ge(s_qps, done)
                load_xp(g, h, s)

            xp_ahead(1, 0, 0, 2)

            def half_steps(u0, n, ffn):
                with sp.Fori(u0, u0 + n) as u:
                    for i in range(2):
                        xp_ahead(u + (3 + i) // 2, (3 + i) % 2, (1 + i) % 2, 4 * u + (4 + 2 * i))
                        if ffn:
                            for c in range(4 * i, 4 * i + 4):
                                next_tile(0, u - u0, c)

            half_steps(0, 3, False)
            first_tiles(0)
            half_steps(3, 9, True)
            half_steps(12, 2, False)
            xp_ahead(15, 1, 1, 2 * 30)

            sp.wait_ge(s_res, 1)
            sp.dma_start(res_d, X2).then_inc(s_resst, 16)
            sp.wait_ge(s_route, 2)

            def conv_matrices(cv):
                with sp.Fori(0, D // 16) as u:
                    for s in range(2):
                        sp.wait_ge(s_cmm, 2 * u + (16 * cv + s + 1))
                        src = bass.AP(kpad[cv].tensor, (2 * u + s) * (8 * 3 * TAPS) + cv,
                                      [[1, P], [3 * TAPS, 8], [1, 2 * P]])
                        sp.dma_start(tp[:, s, :, :], src).then_inc(s_tp[s], 16)

            conv_matrices(0)
            sp.wait_ge(s_cmm, 16 + CR)
            first_tiles(1)
            sp.wait_ge(s_cev, 16 + CR)
            sp.wait_ge(s_resst, 16)
            with sp.Fori(0, 8) as u:
                for c in range(8):
                    next_tile(1, u, c)
                sp.dma_start(X1[:, ds(1024 * u, 1024)], res_d[:, ds(1024 * u, 1024)]).then_inc(s_resld, 16)
            for c in range(8):
                next_tile(1, 8, c)
            for s in range(4):
                sp.wait_ge(s_w[s], 32 * (NFL // 4) * 2)
                sp.wait_ge(s_xs[s], 16 * (NFL // 4) * 2)
            sp.wait_ge(s_xsT, 2 * (NF + 2) + CR)
            conv_matrices(1)
            for i in range(8):
                sp.wait_ge(s_oev, 2 * i + (2 + CR))
                k, b0 = i // 4, (i % 4) * 8
                sp.dma_start(out_v[:, k, b0:b0 + 8, :], R[:, 8 * i:8 * i + 8, :]).then_inc(s_out, 16)
            sp.wait_ge(s_out, 16 * 8)
            for s in range(4):
                sp.wait_ge(s_st[s], 16 * (2 * NF // 4 + 1))

        @block.gpsimd
        def _(pool):
            pool.memset(prodv[:, 0:ZC], 0.0).then_inc(s_zero, 1)
            pool.wait_ge(s_bo3, 1)
            for layer in range(2):
                pool.dma_start(bo3_d[layer], bout3[:, layer, :]).then_inc(s_bo3st, 16)

            def scatter(layer):
                pool.wait_ge(s_rows, layer + 1)
                pool.wait_ge(s_xn, 16 * (layer + 1))
                if layer == 0:
                    pool.wait_ge(s_zf, 16 * NZ)
                else:
                    for s in range(4):
                        pool.wait_ge(s_xs[s], 16 * (NFL // 4))
                for j in range(NT):
                    for k in range(2):
                        pool.indirect_dma_start(
                            sorted_x, bass.IndirectOffsetOnAxis(ap=idx[:, k, j:j + 1], axis=0),
                            XN[:, j, :], None).then_inc(s_sc, 16)

            def pool_products(b, s, free, count):
                pool.wait_ge(s_qkv, 2 * b + 3)
                pool.wait_ge(free, count)
                for t in range(2):
                    last = qk_product(pool, s, t)
                last.then_inc(s_pp, 1)

            def gather(layer):
                pool.wait_ge(s_sc, 16 * 2 * NT * (layer + 1))
                for s in range(4):
                    pool.wait_ge(s_st[s], 16 * (NF // 4 * (layer + 1) + 1))
                    pool.wait_ge(s_w[s], 32 * (NFL // 4) * (layer + 1))
                    pool.wait_ge(s_xs[s], 16 * (NFL // 4) * (layer + 1))
                for j in range(NT):
                    if layer == 0 and j in (16, 32):
                        b = B2 + j // 8
                        pool_products(b, b % 2, s_on, b - 1)
                    if j % 8 == 0 and j >= 16:
                        pool.wait_ge(s_comb, 8 * layer + j // 8 - 1)
                    for k, dst in ((0, XN[:, j, :]), (1, Y2[:, j % 16, :])):
                        pool.indirect_dma_start(
                            dst, None, sorted_y,
                            bass.IndirectOffsetOnAxis(ap=idx[:, k, j:j + 1], axis=0)).then_inc(s_gy[j // 8 % 2], 16)

            def pool_values(b, s):
                pool.wait_ge(s_qkv, 2 * b + 3)
                pool.wait_ge(s_on, b - 1)
                kv = qkv[:, s, :, D:3 * D].rearrange("p t (g e) -> p t g e", g=H)
                for t in range(2):
                    v = kv[:, t, :, DH:2 * DH].rearrange("p g e -> p e g")
                    last = pool.tensor_tensor(vals[:, s, t, :].rearrange("p (e g) -> p e g", e=DH),
                                              v, ones[:, :].rearrange("p (e g) -> p e g", e=DH), ALU.mult)
                last.then_inc(s_vals, 1)

            scatter(0)
            pool.wait_ge(s_on, B1)
            pool.sem_inc(s_vals, 1)
            pool_values(B1, B1 % 2)
            pool_products(B1 + 1, (B1 + 1) % 2, s_on, B1)
            pool_values(B1 + 1, (B1 + 1) % 2)
            with pool.Fori(0, (B2 - B1 - 2) // 2) as u:
                for i in range(2):
                    b, s = 2 * u + (B1 + 2 + i), (B1 + i) % 2
                    pool_products(b, s, s_sub, b - 1)
                    pool_values(b, s)
            pool_products(B2, B2 % 2, s_sub, B2 - 1)
            gather(0)
            pool.wait_ge(s_xn, 32)
            pool.tensor_tensor(X2, X2, XN[:, :, :].rearrange("p j d -> p (j d)"), ALU.add).then_inc(s_res, 1)
            scatter(1)
            gather(1)

        @block.scalar
        def _(act):
            act.dma_start(w3s[:, :], w32).then_inc(s_w3, 16)
            act.dma_start(rws[:, :], rows).then_inc(s_cst, 16)
            act.dma_start(cst[:, :], consts).then_inc(s_cst, 16)
            act.dma_start(w1s[:, :], w128).then_inc(s_cst, 16)
            for layer in range(2):
                act.dma_start(boutf[:, layer, :], bout_d[layer].rearrange("(a e) d -> a (e d)", a=1)
                              .to_broadcast([3, E * D])).then_inc(s_bf, 16)
            act.sem_inc(s_xt, CR)
            act.sem_inc(s_yev, CR)
            act.sem_inc(s_pev, CR)
            act.sem_inc(s_qkv, 1)
            for s in range(4):
                act.sem_inc(s_st[s], 16)
            for s in range(2):
                act.sem_inc(s_xtst[s], 16)
            act.sem_inc(s_xsT, CR)
            act.sem_inc(s_gelu, CR)
            act.sem_inc(s_hT, CR)
            act.sem_inc(s_cT, CR)
            act.sem_inc(s_cg, CR)

            def copy_xT(layer, u0, u1):
                with act.Fori(u0, u1) as u:
                    for s in range(2):
                        g = 2 * u + (16 * layer + s)
                        act.wait_ge(s_tr, g + (1 + CR))
                        act.wait_ge(s_gate, g + 1)
                        if layer == 0:
                            act.wait_ge(s_xtst[s], 16 * u + 16)
                        act.copy(xT[:, s, :], psH[s][:, :]).then_inc(s_xt, 1)

            def rows_T(layer, v, c):
                s = c % 2
                F = 8 * v + (c + layer * NF)
                act.wait_ge(s_XT, F + (2 * layer + 1))
                act.wait_ge(s_H, 2 * F + 2)
                act.copy(xsT[:, s, :], psT[:, 0:FT]).then_inc(s_xsT, 1)

            def next_rows_T(layer, v, c):
                if c < 6:
                    rows_T(layer, v, c + 2)
                else:
                    rows_T(layer, v + 1, c - 6)

            def gelus(layer, v, c):
                s = c % 2
                F = 8 * v + (c + layer * NF)
                act.wait_ge(s_Y, F + 1)
                for m in range(MK):
                    if m % 2 == 0:
                        act.wait_ge(s_H, 2 * F + (5 + m // 2))
                    g = act.activation(hT[:, s, m, :], psH[2 * s + m // 2][:, (m % 2) * FT:(m % 2 + 1) * FT],
                                       ACT.Gelu, bias=wc[:, c % 4, HID + MK * D + m:HID + MK * D + m + 1])
                g.then_inc(s_gelu, 1)

            def expert_evac(layer, v, c):
                F = 8 * v + (c + layer * NF)
                stored = 32 * v + 16 * (c // 4 + layer * (NF // 4) + 1)
                act.wait_ge(s_Y, F + (1 + CR))
                act.wait_ge(s_st[c % 4], stored)
                act.copy(ys[:, c % 4, :], psY[:, 0:FT]).then_inc(s_yev, 1)

            def evac_qkv(m, s, t, pool_read=False, bank=psQ):
                act.wait_ge(s_qps, 2 * m + (t + 1))
                if t == 0 and pool_read:
                    act.wait_ge(s_vals, m - B1)
                elif t == 0 and not (isinstance(m, int) and m < 2):
                    act.wait_ge(s_on, m - 1)
                act.copy(qkv[:, s, t, :], bank[:, 0:3 * D]).then_inc(s_qkv, 1)

            def std_dev(n):
                act.wait_ge(s_var, n)
                act.activation(sdev[:, :], var[:, :], ACT.Sqrt).then_inc(s_rstd, 1)

            def pair_heads(b):
                act.wait_ge(s_ot, b + 1)
                act.copy(OT, psA[:, 0:256]).then_inc(s_otsb, 1)

            def pair_exp(b, s):
                act.wait_ge(s_sub, b + 1)
                act.activation(S[:, s, :], S[:, s, :], ACT.Exp, scale=SCALE).then_inc(s_exp, 1)

            def scale_experts(i, par, gathered):
                act.wait_ge(s_gy[par], gathered)
                for c in range(8):
                    j = 8 * i + c
                    y1 = XN[:, ds(j, 1), :].rearrange("p a d -> p (a d)")
                    act.activation(y1, y1, ACT.Copy, scale=wt[:, 0, ds(j, 1)])
                    y2 = Y2[:, 8 * par + c, :]
                    t = act.activation(y2, y2, ACT.Copy, scale=wt[:, 1, ds(j, 1)])
                t.then_inc(s_scaled, 1)

            def half_step(b, s):
                if not (isinstance(b, int) and b == 1):
                    pair_heads(b - 1)
                evac_qkv(b + 1, s, 0)
                evac_qkv(b + 1, s, 1)
                pair_exp(b, 1 - s)

            def half_steps(u0, n, ffn, comb=False):
                with act.Fori(u0, u0 + n) as u:
                    for i in range(2):
                        b, s = 2 * u + (1 + i), i % 2
                        if ffn:
                            for c in range(4 * i, 4 * i + 4):
                                gelus(0, u - u0, c)
                                if c % 4 == 0:
                                    pair_heads(b - 1)
                                if c > 0:
                                    expert_evac(0, u - u0, c - 1)
                                if c == 7:
                                    expert_evac(0, u - u0, 7)
                                if c % 4 < 2:
                                    evac_qkv(b + 1, s, c % 4, pool_read=True)
                                if c % 4 == 3:
                                    pair_exp(b, 1 - s)
                                next_rows_T(0, u - u0, c)
                        else:
                            half_step(b, s)
                        if comb:
                            scale_experts(2 * u + (i - 2 * u0), i, 256 * u + 256 * (1 - u0))

            std_dev(1)
            copy_xT(0, 0, 6)
            for t in range(2):
                evac_qkv(0, 0, t, bank=psA)
            copy_xT(0, 6, NT // 8)
            pair_exp(0, 0)
            act.wait_ge(s_rin, 1)
            act.activation(best[:, 4, :], best[:, 4, :], ACT.Exp).then_inc(s_ex, 1)
            for t in range(2):
                evac_qkv(1, 1, t)
            for b in (1, 2):
                half_step(b, (b + 1) % 2)
            half_steps(1, 2, False)
            rows_T(0, 0, 0)
            rows_T(0, 0, 1)
            half_steps(3, 9, True)
            half_steps(12, 3, False, comb=True)
            pair_heads(NPAIR - 2)
            pair_exp(NPAIR - 1, 1)
            scale_experts(6, 0, 256 * 4)
            pair_heads(NPAIR - 1)
            pair_heads(NPAIR)
            scale_experts(7, 1, 256 * 4)
            std_dev(2)
            copy_xT(1, 0, 6)
            std_dev(3)
            copy_xT(1, 6, NT // 8)

            def affine(u, s):
                act.wait_ge(s_htr, 2 * u + (s + 1 + CR))
                act.wait_ge(s_pps, 8 * u + 4 * (s + 1))
                aff = dict(scale=w1s[:, W_GAM:W_GAM + 1], bias=w1s[:, W_BET:W_BET + 1])
                act.activation(xT[:, s, :], psH[s][:, :], ACT.Identity, **aff)
                act.activation(xTr[:, s, :].rearrange("p (k n) -> p k n", k=4),
                               psH[s][:, :].rearrange("p (k n) -> p k n", k=4)[:, :, ::-1],
                               ACT.Identity, **aff).then_inc(s_hT, 1)

            affine(0, 0)
            for g in range(NT // 4):
                if g + 1 < NT // 4:
                    affine((g + 1) // 2, (g + 1) % 2)
                if g == 0:
                    act.wait_ge(s_rin, 2)
                    lg = rt[7].rearrange("p j e -> p (j e)")
                    act.activation(lg, lg, ACT.Exp).then_inc(s_ex, 1)
                    act.wait_ge(s_resst, 16)
                for j in range(4 * g, 4 * g + 4):
                    act.wait_ge(s_pps, j + 1 + 8)
                    act.copy(VX1j[:, j, :], psH[2 + j % 2][:, 0:2 * D])
                    act.copy(X2j[:, j, :], psH[2 + j % 2][:, 2 * D:3 * D]).then_inc(s_pev, 1)
            rows_T(1, 0, 0)
            rows_T(1, 0, 1)
            with act.Fori(0, NF // 8) as u:
                for c in range(8):
                    gelus(1, u, c)
                    if c > 0:
                        expert_evac(1, u, c - 1)
                    if c == 7:
                        expert_evac(1, u, 7)
                    next_rows_T(1, u, c)
            act.wait_ge(s_cev, 32 + CR)

            def collect(u, s):
                act.wait_ge(s_ctr, 2 * u + (s + 1))
                act.copy(xg[:, s, :].rearrange("p (j d) -> p j d", j=4), Vj[:, ds(8 * u + 4 * s, 4), :])\
                    .then_inc(s_cg, 1)

            def out_T(u, s):
                act.wait_ge(s_ctr, 2 * u + (s + 1 + CR))
                act.wait_ge(s_ops, 2 * u + (s + 1))
                act.copy(xT[:, s, :], psH[s][:, :]).then_inc(s_cT, 1)

            collect(0, 0)
            with act.Fori(0, NT // 8 - 1) as u:
                collect(u, 1)
                out_T(u, 0)
                collect(u + 1, 0)
                out_T(u, 1)
            collect(NT // 8 - 1, 1)
            out_T(NT // 8 - 1, 0)
            out_T(NT // 8 - 1, 1)

        @block.tensor
        def _(pe):
            pe.wait_ge(s_cst, 48)
            pe.wait_ge(s_w3, 16)
            pe.wait_ge(s_set, 1)
            pe.matmul(psT[:, 0:2 * D], w3s[:, 0:P], w3s[:, P:P + 2 * D], start=True, stop=True).then_inc(s_wps, 1)
            one = ones[0:1, :]
            pe.matmul(psY[:, 0:D], one, rws[:, R_BQ:R_BQ + D], start=True, stop=True)
            pe.matmul(psY[:, D:3 * D], bdn[:, :], w3s[:, P:P + 2 * D], start=True, stop=False)
            pe.matmul(psY[:, D:3 * D], one, rws[:, R_BUP:R_BUP + 2 * D], start=False, stop=True)
            pe.matmul(psH[2][:, 0:D], one, rws[:, R_BO0:R_BO0 + D], start=True, stop=True)
            pe.matmul(psH[2][:, D:2 * D], one, rws[:, R_BO1:R_BO1 + D], start=True, stop=True)
            pe.matmul(psH[3][:, 0:3 * D], one, rws[:, R_BIN1:R_BIN1 + 3 * D], start=True, stop=True)\
                .then_inc(s_bps, 1)
            pe.sem_inc(s_tr, CR)
            pe.sem_inc(s_gate, CR)
            pe.sem_inc(s_H, 2 * CR)
            pe.sem_inc(s_Y, CR)
            pe.sem_inc(s_ot, 1)
            pe.sem_inc(s_htr, CR)
            pe.sem_inc(s_pps, 8)
            pe.sem_inc(s_cmm, CR)
            pe.sem_inc(s_ctr, CR)
            pe.sem_inc(s_ops, CR)

            def transposes_and_gates(layer, wg):
                if layer == 1:
                    pe.wait_ge(s_xup, NPAIR + 1)
                    pe.wait_ge(s_qkv, 2 * NPAIR + 1)

                def gates(g):
                    pe.wait_ge(s_xt, 16 * layer + g + 1 + CR)
                    for k in range(4):
                        j = 4 * g + k
                        t = pe.matmul(psQ[:, j * E:(j + 1) * E], xT[:, g % 2, k * P:(k + 1) * P],
                                      w1s[:, wg:wg + E], start=True, stop=True)
                    t.then_inc(s_gate, 1)

                for g in range(NT // 4):
                    if layer == 0 and g == 12:
                        pe.wait_ge(s_set, 2)
                        for t in range(2):
                            qkv_tile(0, 0, t, 16, bank=psA)
                    pe.wait_ge(s_xn, 16 * layer + g + 1)
                    pe.wait_ge(s_xt, 16 * layer + g + 1)
                    for k in range(4):
                        t = pe.transpose(psH[g % 2][:, k * P:(k + 1) * P], XN[:, 4 * g + k, :], ident)
                    t.then_inc(s_tr, 1)
                    if g > 0:
                        gates(g - 1)
                gates(NT // 4 - 1)

            def route_counts(layer):
                pe.wait_ge(s_rank, layer + 1)
                pe.matmul(psA[:, 0:E], tri, small[:, 0, :], start=True, stop=True)
                pe.matmul(psA[:, E:2 * E], ones[:, :], small[:, 0, :], start=True, stop=True).then_inc(s_tot, 1)

            def rows_X(layer, v, c):
                F = 8 * v + (c + layer * NF)
                loads = 32 * v + 16 * (c // 4 + 1 + layer * (NFL // 4))
                pe.wait_ge(s_xs[c % 4], loads)
                pe.wait_ge(s_xsT, F + (2 * layer + CR))
                for r in range(FR):
                    t = pe.transpose(psT[:, r * P:(r + 1) * P],
                                     xs[:, c % 4, r * P:(r + 1) * P], ident)
                t.then_inc(s_XT, 1)

            def next_rows_X(layer, v, c):
                if c < 7:
                    rows_X(layer, v, c + 1)
                else:
                    rows_X(layer, v + 1, 0)

            def hidden(layer, v, c):
                s = c % 2
                F = 8 * v + (c + layer * NF)
                loads = 64 * v + 32 * (c // 4 + 1 + layer * (NFL // 4))
                pe.wait_ge(s_w[c % 4], loads)
                pe.wait_ge(s_xsT, F + (2 * layer + 1 + CR))
                pe.wait_ge(s_gelu, F + 1)
                for m in range(MK):
                    t = pe.matmul(psH[2 * s + m // 2][:, (m % 2) * FT:(m % 2 + 1) * FT],
                                  wc[:, c % 4, m * P:(m + 1) * P], xsT[:, s, :], start=True, stop=True)
                    if m % 2 == 1:
                        t.then_inc(s_H, 1)

            def expert_out(layer, v, c):
                s = c % 2
                F = 8 * v + (c + layer * NF)
                pe.wait_ge(s_gelu, F + (1 + CR))
                pe.wait_ge(s_yev, F + CR)
                pe.matmul(psY[:, 0:FT].rearrange("p (r d) -> p r d", r=FR), ones3[:, :],
                          bo[:, c % 4, None, :].to_broadcast([3, FR, D]), start=True, stop=False)
                for r in range(FR):
                    for m in range(MK):
                        t = pe.matmul(psY[:, r * P:(r + 1) * P],
                                      hT[:, s, m, r * P:(r + 1) * P],
                                      wc[:, c % 4, HID + m * D:HID + (m + 1) * D],
                                      start=False, stop=(r == FR - 1 and m == MK - 1))
                t.then_inc(s_Y, 1)

            def heads_T(b, s):
                pe.wait_ge(s_on, b)
                pe.wait_ge(s_xup, b)
                for t in range(2):
                    i = pe.transpose(psA[:, t * P:(t + 1) * P], On[:, s, t * P:(t + 1) * P], ident)
                i.then_inc(s_ot, 1)

            def heads_out(b):
                pe.wait_ge(s_otsb, b + 1)
                pe.matmul(psA[:, 256:512].rearrange("p (t d) -> p t d", t=2), ones3[:, :],
                          b3[:, None, B_O0:B_O0 + D].to_broadcast([3, 2, D]), start=True, stop=False)
                for t in range(2):
                    i = pe.matmul(psA[:, 256 + t * P:256 + (t + 1) * P], OT[:, t * P:(t + 1) * P],
                                  w1s[:, W_O0:W_O0 + D], start=False, stop=(t == 1))
                i.then_inc(s_ao, 1)

            def qkv_tile(m, s, t, loads, bank=psQ):
                if t == 0:
                    pe.wait_ge(s_xp[s], loads)
                pe.wait_ge(s_qkv, 2 * m + (t + 1))
                pe.matmul(bank[:, 0:3 * D], ones3[:, :], b3[:, B_QKV:B_QKV + 3 * D], start=True, stop=False)
                pe.matmul(bank[:, 0:3 * D], xp[:, s, t * P:(t + 1) * P], wqkv[:, :], start=False, stop=True)\
                    .then_inc(s_qps, 1)

            def half_step(b, m, s, loads):
                if not (isinstance(b, int) and b == 1):
                    heads_T(b - 1, 1 - s)
                    heads_out(b - 1)
                qkv_tile(m, s, 0, loads)
                qkv_tile(m, s, 1, loads)

            def half_steps(u0, n, ffn):
                with pe.Fori(u0, u0 + n) as u:
                    for i in range(2):
                        b = 2 * u + (1 + i)
                        m, s = b + 1, i % 2
                        loads = 16 * u + 16 * 2
                        if ffn:
                            for c in range(4 * i, 4 * i + 4):
                                next_rows_X(0, u - u0, c)
                                if c % 4 == 0:
                                    heads_T(b - 1, 1 - s)
                                hidden(0, u - u0, c)
                                if c > 0:
                                    expert_out(0, u - u0, c - 1)
                                if c % 4 == 1:
                                    heads_out(b - 1)
                                if c % 4 < 2:
                                    qkv_tile(m, s, c % 4, loads)
                        else:
                            half_step(b, m, s, loads)
                    if ffn:
                        expert_out(0, u - u0, 7)

            transposes_and_gates(0, W_G0)
            route_counts(0)
            pe.wait_ge(s_route, 1)
            for t in range(2):
                qkv_tile(1, 1, t, 16)
            for b in (1, 2):
                half_step(b, b + 1, (b + 1) % 2, 16 * 2)
            half_steps(1, 2, False)
            rows_X(0, 0, 0)
            half_steps(3, 9, True)
            rows_X(0, NF // 8, 1)
            half_steps(12, 3, False)
            for b in (NPAIR - 2, NPAIR - 1, NPAIR):
                heads_T(b, (b - 1) % 2)
                heads_out(b)
            transposes_and_gates(1, W_G1)

            def hn_T(u, s):
                pe.wait_ge(s_hg, 2 * u + (s + 1))
                pe.wait_ge(s_hT, 2 * u + (s + 1))
                for k in range(4):
                    t = pe.transpose(psH[s][:, k * P:(k + 1) * P], xg[:, s, k * P:(k + 1) * P], ident)
                t.then_inc(s_htr, 1)

            def project(u, s):
                pe.wait_ge(s_hT, 2 * u + (s + 1 + CR))
                for k in range(4):
                    pe.wait_ge(s_pev, 8 * u + (4 * s + k + 1))
                    bank = psH[2 + k % 2]
                    pe.matmul(bank[:, 0:3 * D], ones3[:, :], b3[:, B_IN1:B_IN1 + 3 * D], start=True, stop=False)
                    for q, src in ((0, xT), (2, xT), (1, xTr)):
                        t = pe.matmul(bank[:, q * D:(q + 1) * D], src[:, s, k * P:(k + 1) * P],
                                      w1s[:, W_IN1 + q * D:W_IN1 + (q + 1) * D], start=False, stop=(q == 1))
                    t.then_inc(s_pps, 1)

            def two_groups(u):
                hn_T(u, 1)
                project(u, 0)
                hn_T(u + 1, 0)
                project(u, 1)

            hn_T(0, 0)
            for g in range(4):
                if g == 3:
                    route_counts(1)
                hn_T((g + 1) // 2, (g + 1) % 2)
                project(g // 2, g % 2)
            with pe.Fori(2, NT // 8 - 1) as u:
                two_groups(u)
            hn_T(NT // 8 - 1, 1)
            project(NT // 8 - 1, 0)
            project(NT // 8 - 1, 1)
            pe.wait_ge(s_pev, NT + CR)

            def convolution(cv):
                diag = P if cv == 0 else 0
                with pe.Fori(0, 8) as u:
                    for s in range(2):
                        pe.wait_ge(s_tp[s], 16 * u + (16 * 8 * cv + 16))
                        pe.wait_ge(s_cev, 2 * u + (16 * cv + s + 1))
                        for k in range(8):
                            v = V[:, ds(1024 * u + (512 * s + 64 * k), NT)]
                            v0 = V[:, ds(1024 * u + (512 * s + 64 * k), NT // 2)]
                            pe.matmul(psC[s][:, k * NT:(k + 1) * NT], tp[:, s, k, diag:diag + P], v,
                                      start=True, stop=False)
                            t = pe.matmul(psC[s][:, k * NT + NT // 2:(k + 1) * NT],
                                          tp[:, s, k, P - diag:2 * P - diag], v0, start=False, stop=True)
                        t.then_inc(s_cmm, 1)

            convolution(0)
            rows_X(1, 0, 0)
            with pe.Fori(0, NF // 8) as u:
                for c in range(8):
                    next_rows_X(1, u, c)
                    hidden(1, u, c)
                    if c > 0:
                        expert_out(1, u, c - 1)
                expert_out(1, u, 7)
            rows_X(1, NF // 8, 1)
            convolution(1)

            def out_tiles_T(u, s):
                pe.wait_ge(s_cg, 2 * u + (s + 1 + CR))
                pe.wait_ge(s_cT, 2 * u + (s + 1))
                for k in range(4):
                    t = pe.transpose(psH[s][:, k * P:(k + 1) * P], xg[:, s, k * P:(k + 1) * P], ident)
                t.then_inc(s_ctr, 1)

            def out_project(u, s):
                pe.wait_ge(s_cT, 2 * u + (s + 1 + CR))
                pe.wait_ge(s_oev, 2 * u + (s + 1))
                pe.matmul(psH[2 + s][:, :].rearrange("p (k d) -> p k d", k=4), ones3[:, :],
                          b3[:, None, B_O1:B_O1 + D].to_broadcast([3, 4, D]), start=True, stop=False)
                for k in range(4):
                    t = pe.matmul(psH[2 + s][:, k * P:(k + 1) * P], xT[:, s, k * P:(k + 1) * P],
                                  w1s[:, W_O1:W_O1 + D], start=False, stop=(k == 3))
                t.then_inc(s_ops, 1)

            out_tiles_T(0, 0)
            with pe.Fori(0, NT // 8 - 1) as u:
                out_tiles_T(u, 1)
                out_project(u, 0)
                out_tiles_T(u + 1, 0)
                out_project(u, 1)
            out_tiles_T(NT // 8 - 1, 1)
            out_project(NT // 8 - 1, 0)
            out_project(NT // 8 - 1, 1)

        @block.vector
        def _(dve):
            steps = [0]

            def link(ins):
                steps[0] += 1
                ins.then_inc(s_v, 1)
                dve.wait_ge(s_v, steps[0])

            dve.memset(ones[:, :], 1.0)
            link(dve.memset(ones3[:, :], 1.0))
            dve.sem_inc(s_cev, CR)
            dve.sem_inc(s_oev, CR)
            dve.sem_inc(s_xup, 1)
            dve.sem_inc(s_otsb, 1)

            def in_three_parts(dst, src, n):
                link(dve.tensor_copy(partb[:, 0:n], src))
                link(dve.scalar_tensor_tensor(out=part[:, 0:n], in0=partb[:, 0:n], scalar=cst[0:3, C_M1:C_M1 + 1],
                                              in1=src, op0=ALU.mult, op1=ALU.add))
                link(dve.tensor_copy(partb[:, 0:n], part[:, 0:n]))
                link(dve.scalar_tensor_tensor(out=part[:, 0:n], in0=partb[:, 0:n], scalar=cst[0:3, C_M2:C_M2 + 1],
                                              in1=part[:, 0:n], op0=ALU.mult, op1=ALU.add))
                link(dve.tensor_copy(dst, part[:, 0:n]))

            def fused_weights():
                dve.wait_ge(s_wps, 1)
                dve.tensor_copy(wqkv[:, 0:D], w1s[:, W_Q:W_Q + D])
                dve.tensor_copy(wqkv[:, D:3 * D], psT[:, 0:2 * D])
                dve.wait_ge(s_bps, 1)
                dve.tensor_copy(brow[:, 0:3 * D], psY[0:3, 0:3 * D])
                dve.tensor_copy(brow[:, B_O0:B_O0 + 2 * D], psH[2][0:3, 0:2 * D])
                link(dve.tensor_copy(brow[:, B_IN1:B_IN1 + 3 * D], psH[3][0:3, 0:3 * D]))
                in_three_parts(b3[:, :], brow[:, :], B_END)
                dve.sem_inc(s_set, 1)

            def norm_stats(src, n):
                for j in range(NT):
                    if n == 1 and j % 16 == 0:
                        dve.wait_ge(s_x[j // 16], 16)
                    dve.bn_stats(stats[:, j, :], src[:, j, :])
                link(dve.memset(tmp[:, 0:1], 0.0))
                me, qe, mo, qo = (stats[:, :, i] for i in (1, 2, 4, 5))
                dve.tensor_tensor(mean[:, :], me, mo, ALU.add)
                link(dve.tensor_tensor(tmp[:, :], me, mo, ALU.subtract))
                dve.tensor_tensor(var[:, :], qe, qo, ALU.add)
                link(dve.tensor_tensor(tmp[:, :], tmp[:, :], tmp[:, :], ALU.mult))
                dve.tensor_scalar(mean[:, :], mean[:, :], 0.5, None, ALU.mult)
                link(dve.tensor_scalar(tmp[:, :], tmp[:, :], 0.25, EPS, ALU.mult, ALU.add))
                dve.scalar_tensor_tensor(out=var[:, :], in0=var[:, :], scalar=1.0 / D, in1=tmp[:, :],
                                         op0=ALU.mult, op1=ALU.add).then_inc(s_var, 1)
                dve.wait_ge(s_rstd, n)
                link(dve.reciprocal(rstd[:, :], sdev[:, :]))
                link(dve.tensor_tensor(tmp[:, :], rstd[:, :], rstd[:, :], ALU.mult))
                link(dve.tensor_tensor(tmp[:, :], tmp[:, :], var[:, :], ALU.mult))
                link(dve.tensor_scalar(tmp[:, :], tmp[:, :], -0.5, 1.5, ALU.mult, ALU.add))
                link(dve.tensor_tensor(rstd[:, :], rstd[:, :], tmp[:, :], ALU.mult))

            def normalised(dst, src, j):
                return dve.tensor_scalar(dst, src[:, j, :], mean[:, j:j + 1], rstd[:, j:j + 1],
                                         ALU.subtract, ALU.mult)

            def normalise_x():
                for j in range(NT):
                    t = normalised(XN[:, j, :], X, j)
                    if j % 4 == 3:
                        t.then_inc(s_xn, 1)

            rt_L, oh1, oh2, t0, t1, Mk, C, rt_X = rt[0:8]
            m1, m2, k1, k2, ta, tb = (best[:, i, :] for i in range(6))
            base, tot, nt, end, off = (small[:, i, :] for i in range(1, 6))

            def bt(ap, n):
                return ap[:, :, None].to_broadcast([P, NT, n])

            def be(ap):
                return ap[:, None, :].to_broadcast([P, NT, E])

            def route_scores(layer):
                dve.wait_ge(s_gate, 16 * (layer + 1) + CR)
                lg = psQ[:, :].rearrange("p (j e) -> p j e", e=E)
                if layer == 0:
                    link(dve.tensor_copy(rt_L, lg))
                else:
                    link(dve.tensor_copy(rt_X, lg))
                    link(dve.tensor_reduce(m1, rt_X, AX.X, ALU.max))
                    link(dve.tensor_tensor(rt_X, rt_X, bt(m1, E), ALU.subtract))
                    dve.sem_inc(s_rin, 1)

            def route_softmax():
                dve.wait_ge(s_ex, 2)
                link(dve.tensor_reduce(m1, rt_X, AX.X, ALU.add))
                link(dve.reciprocal(m2, m1))
                link(dve.tensor_tensor(rt_L, rt_X, bt(m2, E), ALU.mult))

            def route_best(n):
                m, k, oh = ((m1, k1, oh1), (m2, k2, oh2))[n]
                link(dve.tensor_reduce(m, rt_L, AX.X, ALU.max))
                link(dve.tensor_tensor(t0, rt_L, bt(m, E), ALU.is_equal))
                link(dve.tensor_tensor(t0, t0, be(rank8), ALU.mult))
                link(dve.tensor_reduce(k, t0, AX.X, ALU.max))
                link(dve.tensor_tensor(oh, be(rank8), bt(k, E), ALU.is_equal))
                if n == 0:
                    link(dve.tensor_scalar(t1, oh, BIG, None, ALU.mult))
                    link(dve.tensor_tensor(rt_L, rt_L, t1, ALU.subtract))

            def route_weights(layer):
                if layer == 0:
                    link(dve.tensor_tensor(ta, m2, m1, ALU.subtract))
                    dve.sem_inc(s_rin, 1)
                    dve.wait_ge(s_ex, 1)
                    link(dve.tensor_scalar(tb, ta, 1.0, None, ALU.add))
                    link(dve.reciprocal(wt[:, 0, :], tb))
                    link(dve.tensor_tensor(wt[:, 1, :], ta, wt[:, 0, :], ALU.mult))
                else:
                    link(dve.tensor_tensor(ta, m1, m2, ALU.add))
                    link(dve.tensor_scalar(ta, ta, 1e-9, None, ALU.add))
                    link(dve.reciprocal(tb, ta))
                    dve.tensor_tensor(wt[:, 0, :], m1, tb, ALU.mult)
                    link(dve.tensor_tensor(wt[:, 1, :], m2, tb, ALU.mult))

            def route_ranks():
                link(dve.tensor_tensor(Mk, oh1, oh2, ALU.add))
                for e in range(E):
                    sc = dve.tensor_tensor_scan(C[:, :, e], ones[:, 0:NT], Mk[:, :, e], 0.0, ALU.mult, ALU.add)
                link(sc)
                dve.tensor_copy(small[:, 0, :], C[:, NT - 1, :]).then_inc(s_rank, 1)

            def route_offsets(layer):
                dve.wait_ge(s_tot, layer + 1)
                link(dve.tensor_copy(small[:, 1:3, :].rearrange("p a e -> p (a e)"), psA[:, 0:2 * E]))
                cmp = rcmp[:, 0:E * NTHR].rearrange("p (e q) -> p e q", e=E)
                link(dve.tensor_tensor(cmp, tot[:, :, None].to_broadcast([P, E, NTHR]),
                                       thr[:, None, :].to_broadcast([P, E, NTHR]), ALU.is_gt))
                link(dve.tensor_reduce(nt, cmp, AX.X, ALU.add))
                link(dve.tensor_tensor_scan(end, ones[:, 0:E], nt, 0.0, ALU.mult, ALU.add))
                link(dve.tensor_tensor(off, end, nt, ALU.subtract))
                link(dve.tensor_scalar(off, off, float(FT), -1.0, ALU.mult, ALU.add))
                link(dve.tensor_tensor(off, off, base, ALU.add))
                link(dve.tensor_tensor(C, C, be(off), ALU.add))

            def route_rows():
                for k, oh in ((0, oh1), (1, oh2)):
                    link(dve.tensor_tensor(t0, C, oh, ALU.mult))
                    link(dve.tensor_reduce(ta, t0, AX.X, ALU.add))
                    link(dve.tensor_copy(idx[:, k, :], ta))
                dve.sem_inc(s_rows, 1)
                ecmp = rcmp[:, 0:NFL * E].rearrange("p (f e) -> p f e", e=E)
                link(dve.tensor_tensor(ecmp, iota[:, :, None].to_broadcast([P, NFL, E]),
                                       end[:, None, :].to_broadcast([P, NFL, E]), ALU.is_ge))
                link(dve.tensor_reduce(rt_L.rearrange("p j e -> p (j e)")[:, 0:NFL], ecmp, AX.X, ALU.add))
                dve.tensor_scalar(eid[:, :], rt_L.rearrange("p j e -> p (j e)")[:, 0:NFL], float(E - 1), None,
                                  ALU.min).then_inc(s_route, 1)

            def add_heads(b):
                dve.wait_ge(s_ao, b)
                xv = X[:, ds(2 * b - 2, 2), :].rearrange("p a d -> p (a d)")
                dve.tensor_tensor(xv, xv, psA[:, 256:512], ALU.add).then_inc(s_xup, 1)

            def add_experts(i, par):
                xv = X[:, ds(8 * i, 8), :].rearrange("p a d -> p (a d)")
                dve.wait_ge(s_scaled, i + 1)
                dve.tensor_tensor(xv, xv, XN[:, ds(8 * i, 8), :].rearrange("p a d -> p (a d)"), ALU.add)\
                   .then_inc(s_comb1, 1)
                dve.wait_ge(s_comb1, i + 1)
                dve.tensor_tensor(xv, xv, Y2[:, 8 * par:8 * par + 8, :].rearrange("p a d -> p (a d)"), ALU.add)\
                   .then_inc(s_comb, 1)
                dve.wait_ge(s_comb, i + 1)

            def combine(i, par):
                dve.wait_ge(s_gy[par], 256 * (i // 2 + 5))
                for k in range(2):
                    for c in range(8):
                        j = 8 * i + c
                        t = dve.scalar_tensor_tensor(out=R[:, j, :], in0=Y2[:, 8 * par + c, :] if k else XN[:, j, :],
                                                     scalar=wt[:, k, j:j + 1], in1=R[:, j, :],
                                                     op0=ALU.mult, op1=ALU.add)
                    done = s_comb if k else s_comb1
                    t.then_inc(done, 1)
                    dve.wait_ge(done, i + 9)

            def step(ins):
                ins.then_inc(s_att, 1)

            def scores(b, s, first_step, made=None, on_pool=None):
                if on_pool is not None:
                    dve.wait_ge(s_pp, on_pool)
                else:
                    dve.wait_ge(s_qkv, 2 * b + 3)
                    for t in range(2):
                        i = qk_product(dve, s, t)
                    i.then_inc(s_vp, 1)
                    dve.wait_ge(s_vp, made + 1)
                S3 = S[:, s, :].rearrange("p (n g) -> p n g", g=H)
                step(dve.tensor_reduce(S[:, s, :], prod[:, s, :].rearrange("p (n d) -> p n d", d=DH), AX.X, ALU.add))
                dve.wait_ge(s_att, first_step + 1)
                step(dve.tensor_reduce(Mx, S3, AX.X, ALU.max))
                dve.wait_ge(s_att, first_step + 2)
                dve.tensor_tensor(S3, S3, Mx[:, :, None].to_broadcast([P, 2 * H, H]), ALU.subtract).then_inc(s_sub, 1)

            def weighted(b, s, first_step, skewed=False):
                if skewed:
                    dve.wait_ge(s_vals, b - (B1 - 2))
                dve.wait_ge(s_exp, b + 1)
                step(dve.tensor_reduce(Sm, S[:, s, :].rearrange("p (n g) -> p n g", g=H), AX.X, ALU.add))
                dst = prodv if skewed else prod[:, s, :]
                for t in range(2):
                    if skewed:
                        v = vals[:, s, t, :].rearrange("p (e g) -> p e g", e=DH)
                    else:
                        kv = qkv[:, s, t, D:3 * D].rearrange("p (g e) -> p g e", g=H)
                        v = kv[:, :, DH:2 * DH].rearrange("p g e -> p e g")
                    i = dve.tensor_tensor(
                        dst[:, t * 2048:(t + 1) * 2048].rearrange("p (h e g) -> p h e g", h=H, e=DH),
                        S[:, s, t * 256:(t + 1) * 256].rearrange("p (h g) -> p h g", h=H)[:, :, None, :]
                        .to_broadcast([P, H, DH, H]),
                        v[:, None, :, :].to_broadcast([P, H, DH, H]), ALU.mult)
                dve.wait_ge(s_att, first_step + 1)
                dve.reciprocal(Rc, Sm)
                step(i)
                dve.wait_ge(s_att, first_step + 2)
                step(dve.tensor_reduce(O, dst.rearrange("p (n g) -> p n g", g=H), AX.X, ALU.add))
                dve.wait_ge(s_att, first_step + 3)
                if not (isinstance(b, int) and b == 0):
                    dve.wait_ge(s_ot, b)
                dve.tensor_tensor(On[:, s, :].rearrange("p (n e) -> p n e", e=DH),
                                  O.rearrange("p (n e) -> p n e", e=DH),
                                  Rc[:, :, None].to_broadcast([P, 2 * H, DH]), ALU.mult).then_inc(s_on, 1)

            def pair(b, s, made=None, with_heads=True, combines=None, on_pool=None):
                scores(b, s, K_ATT * b, made, on_pool)
                if with_heads:
                    add_heads(b - 1)
                weighted(b, s, K_ATT * b + 2)
                if combines is not None:
                    add_experts(*combines)

            def skewed_step(b, s):
                scores(b, s, K_ATT * b - 3, on_pool=b - B1)
                weighted(b - 1, 1 - s, K_ATT * b - 1, skewed=True)
                add_heads(b - 1)

            dve.wait_ge(s_w3, 16)
            dve.tensor_copy(bdn[:, :], w3s[:, P + 2 * D:P + 2 * D + 1].to_broadcast([LAT, P])).then_inc(s_set, 1)
            norm_stats(X, 1)
            normalise_x()
            dve.wait_ge(s_cst, 48)
            dve.wait_ge(s_bf, 32)
            fused_weights()
            for layer in range(2):
                in_three_parts(bout3[:, layer, :], boutf[:, layer, :], E * D)
            dve.sem_inc(s_bo3, 1)
            scores(0, 0, 0, made=0)
            dve.wait_ge(s_bo3st, 32)
            route_scores(0)
            route_best(0)
            route_best(1)
            route_weights(0)
            route_ranks()
            route_offsets(0)
            route_rows()
            weighted(0, 0, 2)
            for b in (1, 2):
                pair(b, b % 2, made=b, with_heads=(b == 2))
            with dve.Fori(1, 3) as u:
                for i in range(2):
                    pair(2 * u + (1 + i), (1 + i) % 2, made=2 * u + (1 + i))
            scores(B1, B1 % 2, K_ATT * B1, made=B1)
            add_heads(B1 - 1)
            dve.wait_ge(s_zf, 16 * NZ)
            with dve.Fori(0, (B2 - B1 - 2) // 2) as u:
                for i in range(2):
                    skewed_step(2 * u + (B1 + 1 + i), (B1 + 1 + i) % 2)
            skewed_step(B2 - 1, (B2 - 1) % 2)
            weighted(B2 - 1, (B2 - 1) % 2, K_ATT * B2 - 3, skewed=True)
            with dve.Fori(0, 3) as u:
                pair(2 * u + B2, 1, combines=(2 * u, 0), on_pool=u + (B2 - B1))
                pair(2 * u + (B2 + 1), 0, made=u + (B1 + 1), combines=(2 * u + 1, 1))
            pair(NPAIR - 1, 1, made=B1 + 4, combines=(6, 0))
            add_heads(NPAIR - 1)
            add_heads(NPAIR)
            dve.wait_ge(s_xup, NPAIR + 1)
            add_experts(7, 1)

            norm_stats(X, 2)
            normalise_x()
            dve.wait_ge(s_xn, 32)
            norm_stats(XN, 3)

            def hn_group(g):
                dve.wait_ge(s_htr, g + 1)
                for k in range(4):
                    t = normalised(xg[:, g % 2, k * D:(k + 1) * D], XN, 4 * g + k)
                t.then_inc(s_hg, 1)

            routing = {1: lambda: (route_scores(1), route_softmax()), 2: lambda: route_best(0),
                       3: lambda: route_best(1), 4: route_ranks,
                       5: lambda: route_offsets(1), 6: route_rows, 7: lambda: route_weights(1)}
            for g in range(NT // 4):
                hn_group(g)
                if g in routing:
                    routing[g]()
            dve.wait_ge(s_pev, NT + CR)

            def conv_gate(cv, n, bank, gate):
                dve.wait_ge(s_cmm, n + (16 * cv + 1 + CR))
                sl = ds(512 * n, 512)
                dve.tensor_tensor(V[:, sl], psC[bank][:, :], gate[:, sl], ALU.mult).then_inc(s_cev, 1)

            with dve.Fori(0, 8) as u:
                for s in range(2):
                    conv_gate(0, 2 * u + s, s, X1)
            dve.wait_ge(s_resld, 128)
            combine_after = {1: 0, 4: 1, 6: 2, 9: 3, 11: 4, 14: 5}
            for n in range(D // 8):
                conv_gate(1, n, n % 2, X2)
                if n in combine_after:
                    combine(combine_after[n], combine_after[n] % 2)

            def block_out(u):
                for s in range(2):
                    dve.wait_ge(s_ops, 2 * u + (s + 1 + CR))
                    rv = R[:, ds(8 * u + 4 * s, 4), :].rearrange("p a d -> p (a d)")
                    dve.tensor_tensor(rv, rv, psH[2 + s][:, :], ALU.add).then_inc(s_oev, 1)

            combine(6, 0)
            with dve.Fori(0, 7) as u:
                block_out(u)
            combine(7, 1)
            block_out(7)


def kernel(**inputs):
    import numpy as _np
    import concourse.bacc as _bacc
    from concourse import mybir as _mybir
    from concourse.bass_utils import run_bass_kernel_spmd as _run

    a = {k: _np.asarray(v) for k, v in inputs.items()}
    consts = _np.concatenate([
        _np.eye(P), _np.triu(_np.ones((P, P)), 1), _np.tile(_np.arange(E, 0, -1), (P, 1)),
        _np.tile(FT * _np.arange(NTHR), (P, 1)), _np.tile(_np.arange(NFL), (P, 1)),
        -1.0 * (_np.arange(P)[:, None] >= [[1, 2]])], 1).astype(_np.float32)

    def experts(w_in, b_in, w_out):
        return _np.concatenate([w_in, w_out.reshape(E, MK, P, D).transpose(0, 2, 1, 3).reshape(E, P, MK * D),
                                b_in.reshape(E, MK, P).transpose(0, 2, 1)], 2)

    def padded(k):
        return _np.pad(k, ((0, 0), (TAPS, TAPS)))

    arrays = {
        "x": a["L0_attn_x"],
        "consts": consts,
        "w128": _np.concatenate([a["L0_attn_Wq"], a["L0_ffn_W_gate"], a["L0_attn_Wout"], a["L1_attn_W_in"],
                                 a["L1_ffn_gate_w"].T, a["L1_attn_W_out"], a["L1_attn_gamma"][:, None],
                                 a["L1_attn_beta"][:, None]], 1),
        "w32": _np.concatenate([a["L0_attn_Wdown"].T, a["L0_attn_Wup"], a["L0_attn_bdown"][:, None]], 1),
        "rows": _np.concatenate([a["L0_attn_bq"], a["L0_attn_bup"], a["L0_attn_bout"], a["L1_attn_b_in"],
                                 a["L1_attn_b_out"]])[None, :],
        "moe0": experts(a["L0_ffn_W_in"], a["L0_ffn_b_in"], a["L0_ffn_W_out"]),
        "bout0": a["L0_ffn_b_out"],
        "moe1": experts(a["L1_ffn_w1"], a["L1_ffn_b1"], a["L1_ffn_w2"]),
        "bout1": a["L1_ffn_b2"],
        "kpad0": padded(a["L1_attn_k0"][0, :, ::-1]),
        "kpad1": padded(a["L1_attn_k1"][0]),
    }
    nc = _bacc.Bacc("TRN2", target_bir_lowering=False, num_devices=1)
    arrays = {f"in_{k}": _np.ascontiguousarray(v) for k, v in arrays.items()}
    args = [nc.dram_tensor(k, v.shape, _mybir.dt.from_np(v.dtype), kind="ExternalInput").ap()
            for k, v in arrays.items()]
    out = nc.dram_tensor("out_0", (BATCH, TIME, D), _mybir.dt.float32, kind="ExternalOutput").ap()
    mixed_layers(nc, *args, out)
    return _run(nc, [arrays], core_ids=[0]).results[0]["out_0"]
```
